# Optimizing a Trainium2 kernel written in Bass

```python
import numpy as np
import jax
import jax.numpy as jnp

def _softmax(x, axis=-1):
    return jax.nn.softmax(x, axis=axis)

def _gelu(x):
    return jax.nn.gelu(x, approximate=True)

def _silu(x):
    return jax.nn.silu(x)

def _sigmoid(x):
    return jax.nn.sigmoid(x)

def _layernorm(x, axis=-1, eps=1e-05):
    m = jnp.mean(x, axis=axis, keepdims=True)
    v = jnp.var(x, axis=axis, keepdims=True)
    return (x - m) / jnp.sqrt(v + eps)

def _scatter_add(tgt, idx, src, axis=0):
    return tgt.at[idx].add(src)

def _segment_sum(src, seg, n):
    return jax.ops.segment_sum(src, seg, n)
kernel_name = 'mk_xattn_seq_d4_seqx_r4_aea38b'

def setup_inputs(seed: int=0):
    np.random.seed(seed)
    _w = jnp.asarray

    def _rec_inputs():
        import jax
        import jax.numpy as jnp
        _rk = jax.random.key(seed)
        x = -0.0002928 + 1 * jax.random.normal(jax.random.fold_in(_rk, 1), (64, 128, 256), jnp.float32)
        _lenS = 128 - jax.random.randint(jax.random.fold_in(_rk, 7), (64,), 0, max(1, 128 // 4) + 1, jnp.int32)
        _lenS2 = 128 - jax.random.randint(jax.random.fold_in(_rk, 8), (64,), 0, max(1, 128 // 4) + 1, jnp.int32)
        _ctx_1024P = jax.random.normal(jax.random.fold_in(_rk, 11), (64, 16, 256), jnp.float32)
        _ctx_1024c = jax.random.dirichlet(jax.random.fold_in(_rk, 511), 0.3 * jnp.ones((16,), jnp.float32), (64, 128))
        _ctx_1024t = jnp.einsum('bsk,bkd->bsd', _ctx_1024c, _ctx_1024P)
        _ctx_1024t = _ctx_1024t * jax.lax.rsqrt(jnp.mean(jnp.square(_ctx_1024t)) + 1e-12) * 0.953939
        ctx_1024 = -1.39393e-06 + 0.999914 * (_ctx_1024t + 0.3 * jax.random.normal(jax.random.fold_in(_rk, 611), (64, 128, 256), jnp.float32))
        _validS = jnp.arange(128)[None, :] < _lenS[:, None]
        _validS2 = jnp.arange(128)[None, :] < _lenS2[:, None]
        _causal = jnp.tril(jnp.ones((128, 128), dtype=bool))
        mask_Bx1xSxS2_ff0 = jnp.where(jnp.ones((64, 1, 128, 128), dtype=bool), 0.0, -1000000000.0).astype(jnp.float32)
        mask_Bx1xSxS2_fk0 = jnp.where(jnp.broadcast_to(_validS2[:, None, None, :], (64, 1, 128, 128)), 0.0, 1.0).astype(jnp.float32)
        return (x, ctx_1024, mask_Bx1xSxS2_ff0, mask_Bx1xSxS2_fk0)
    x, ctx_1024, mask_Bx1xSxS2_ff0, mask_Bx1xSxS2_fk0 = _rec_inputs()

    def _L0_xattn_setup():
        import jax, jax.numpy as jnp
        import numpy as np
        EPS = 1e-05

        def _layernorm(x, g, b):
            m = jnp.mean(x, axis=-1, keepdims=True)
            v = jnp.mean((x - m) ** 2, axis=-1, keepdims=True)
            return (x - m) / jnp.sqrt(v + EPS) * g + b

        def _mha(x, kv, Wq, Wk, Wv, mask, causal):
            m = mask[:, None]
            Q = jnp.einsum('bsd,hdk->bhsk', x, Wq) * m
            K = jnp.einsum('bsd,hdk->bhsk', kv, Wk) * m
            V = jnp.einsum('bsd,hdk->bhsk', kv, Wv) * m
            energy = jnp.einsum('bhsk,bhtk->bhst', Q, K)
            S = energy.shape[-1]
            lengths = jnp.sum(energy[:, :, 0, :] != 0, axis=-1)
            cols = jnp.arange(S)
            energy = jnp.where(cols[None, None, None, :] >= lengths[:, :, None, None], -jnp.inf, energy)
            if causal:
                energy = jnp.where(cols[None, :] > cols[:, None], -jnp.inf, energy)
            dk = Wq.shape[-1]
            score = jax.nn.softmax(energy / jnp.sqrt(jnp.asarray(dk, energy.dtype)), axis=-1)
            out = jnp.einsum('bhst,bhtk->bhsk', score, V) * m
            B, H, Sx, dkk = out.shape
            return out.transpose(0, 2, 1, 3).reshape(B, Sx, H * dkk)
        key = jax.random.key(seed)
        ks = jax.random.split(key, 20)
        B, S, D, H = (2, 512, 256, 16)
        dk = D // H
        sd = 0.02
        inp = {'x': jax.random.normal(ks[0], (B, S, D), jnp.float32), 'context': jax.random.normal(ks[1], (B, S, D), jnp.float32), 'Wq1': jax.random.normal(ks[2], (H, D, dk), jnp.float32) * sd, 'Wk1': jax.random.normal(ks[3], (H, D, dk), jnp.float32) * sd, 'Wv1': jax.random.normal(ks[4], (H, D, dk), jnp.float32) * sd, 'Wq2': jax.random.normal(ks[5], (H, D, dk), jnp.float32) * sd, 'Wk2': jax.random.normal(ks[6], (H, D, dk), jnp.float32) * sd, 'Wv2': jax.random.normal(ks[7], (H, D, dk), jnp.float32) * sd, 'ln1_g': jnp.ones((D,), jnp.float32), 'ln1_b': jnp.zeros((D,), jnp.float32), 'ln2_g': jnp.ones((D,), jnp.float32), 'ln2_b': jnp.zeros((D,), jnp.float32), 'ln3_g': jnp.ones((D,), jnp.float32), 'ln3_b': jnp.zeros((D,), jnp.float32), 'fc1_w': jax.random.normal(ks[8], (D, D), jnp.float32) * sd, 'fc1_b': jnp.zeros((D,), jnp.float32), 'fc2_w': jax.random.normal(ks[9], (D, D), jnp.float32) * sd, 'fc2_b': jnp.zeros((D,), jnp.float32)}
        return inp
    _L0_xattn_all = _L0_xattn_setup()
    _L0_xattn_in = {k: v for k, v in _L0_xattn_all.items() if k in ('Wq1', 'Wk1', 'Wv1', 'Wq2', 'Wk2', 'Wv2', 'ln1_g', 'ln1_b', 'ln2_g', 'ln2_b', 'ln3_g', 'ln3_b', 'fc1_w', 'fc1_b', 'fc2_w', 'fc2_b')}
    del _L0_xattn_all

    def _L1_xattn_setup():
        import jax, jax.numpy as jnp
        import numpy as np
        import math
        H, NH, NKV, HD, FF = (256, 16, 4, 64, 1024)
        B, S = (2, 512)
        EPS, THETA = (1e-06, 10000.0)

        def _rmsnorm(x, w, eps=EPS):
            v = jnp.mean(x.astype(jnp.float32) ** 2, axis=-1, keepdims=True)
            return (x.astype(jnp.float32) * jax.lax.rsqrt(v + eps)).astype(x.dtype) * w

        def _rope_tables(seq_len, head_dim, theta=THETA):
            inv_freq = 1.0 / theta ** (jnp.arange(0, head_dim, 2, dtype=jnp.float32) / head_dim)
            freqs = jnp.arange(seq_len, dtype=jnp.float32)[:, None] * inv_freq[None, :]
            emb = jnp.concatenate([freqs, freqs], axis=-1)
            return (jnp.cos(emb), jnp.sin(emb))

        def _rotate_half(x):
            x1, x2 = jnp.split(x, 2, axis=-1)
            return jnp.concatenate([-x2, x1], axis=-1)

        def _apply_rope(x, cos, sin):
            return x * cos[None, None] + _rotate_half(x) * sin[None, None]
        key = jax.random.key(seed)
        ks = jax.random.split(key, 12)
        std = 0.02
        return {'hidden_states': jax.random.normal(ks[0], (B, S, H), jnp.float32), 'kv_states': jax.random.normal(ks[1], (B, S, H), jnp.float32), 'attention_mask': jnp.zeros((B, 1, S, S), jnp.float32), 'ln1_w': jnp.ones((H,), jnp.float32), 'ln2_w': jnp.ones((H,), jnp.float32), 'Wq': jax.random.normal(ks[2], (H, NH * HD), jnp.float32) * std, 'Wk': jax.random.normal(ks[3], (H, NKV * HD), jnp.float32) * std, 'Wv': jax.random.normal(ks[4], (H, NKV * HD), jnp.float32) * std, 'Wo': jax.random.normal(ks[5], (NH * HD, H), jnp.float32) * std, 'Wgate': jax.random.normal(ks[6], (H, FF), jnp.float32) * std, 'Wup': jax.random.normal(ks[7], (H, FF), jnp.float32) * std, 'Wdown': jax.random.normal(ks[8], (FF, H), jnp.float32) * std}
    _L1_xattn_all = _L1_xattn_setup()
    _L1_xattn_in = {k: v for k, v in _L1_xattn_all.items() if k in ('ln1_w', 'ln2_w', 'Wq', 'Wk', 'Wv', 'Wo', 'Wgate', 'Wup', 'Wdown')}
    del _L1_xattn_all

    def _L2_xattn_setup():
        import jax, jax.numpy as jnp
        import numpy as np
        DIM = 256
        N_HEADS = 16
        HEAD_DIM = DIM // N_HEADS
        LN_EPS = 1e-05

        def layer_norm(x, gamma, beta):
            mu = jnp.mean(x, axis=-1, keepdims=True)
            var = jnp.var(x, axis=-1, keepdims=True)
            return (x - mu) * jax.lax.rsqrt(var + LN_EPS) * gamma + beta
        key = jax.random.key(seed)
        ks = jax.random.split(key, 12)
        B, Nq, Nc, D = (2, 512, 512, DIM)
        s = 1.0 / np.sqrt(D)
        return {'query': jax.random.normal(ks[0], (B, Nq, D), jnp.float32), 'context': jax.random.normal(ks[1], (B, Nc, D), jnp.float32), 'Wq': jax.random.normal(ks[2], (D, D), jnp.float32) * s, 'bq': jnp.zeros((D,), jnp.float32), 'Wk': jax.random.normal(ks[3], (D, D), jnp.float32) * s, 'bk': jnp.zeros((D,), jnp.float32), 'Wv': jax.random.normal(ks[4], (D, D), jnp.float32) * s, 'bv': jnp.zeros((D,), jnp.float32), 'Wo': jax.random.normal(ks[5], (D, D), jnp.float32) * s, 'bo': jnp.zeros((D,), jnp.float32), 'gq': jnp.ones((D,), jnp.float32), 'betaq': jnp.zeros((D,), jnp.float32), 'gkv': jnp.ones((D,), jnp.float32), 'betakv': jnp.zeros((D,), jnp.float32)}
    _L2_xattn_all = _L2_xattn_setup()
    _L2_xattn_in = {k: v for k, v in _L2_xattn_all.items() if k in ('Wq', 'bq', 'Wk', 'bk', 'Wv', 'bv', 'Wo', 'bo', 'gq', 'betaq', 'gkv', 'betakv')}
    del _L2_xattn_all

    def _L3_xattn_setup():
        import jax, jax.numpy as jnp
        import numpy as np
        ALPHA = 0.5
        SCORES_CLAMP = 50.0
        LN_EPS = 1e-05
        N_HEADS = 16
        key = jax.random.key(seed)
        ks = jax.random.split(key, 16)
        B, Q, K, D = (2, 512, 512, 256)
        s = 1.0 / np.sqrt(D)
        return {'query': jax.random.normal(ks[0], (B, Q, D), jnp.float32), 'key_in': jax.random.normal(ks[1], (B, K, D), jnp.float32), 'mask': jax.random.randint(ks[2], (B, 1, Q, K), 0, 2).astype(jnp.float32), 'Wq': jax.random.normal(ks[3], (D, D), jnp.float32) * s, 'bq': jnp.zeros((D,), jnp.float32), 'Wk': jax.random.normal(ks[4], (D, D), jnp.float32) * s, 'bk': jnp.zeros((D,), jnp.float32), 'Wv': jax.random.normal(ks[5], (D, D), jnp.float32) * s, 'bv': jnp.zeros((D,), jnp.float32), 'Wo': jax.random.normal(ks[6], (D, D), jnp.float32) * s, 'bo': jnp.zeros((D,), jnp.float32), 'gamma': jnp.ones((D,), jnp.float32), 'beta': jnp.zeros((D,), jnp.float32)}
    _L3_xattn_all = _L3_xattn_setup()
    _L3_xattn_in = {k: v for k, v in _L3_xattn_all.items() if k in ('Wq', 'bq', 'Wk', 'bk', 'Wv', 'bv', 'Wo', 'bo', 'gamma', 'beta')}
    del _L3_xattn_all
    return {'x': x, 'ctx_1024': ctx_1024, 'mask_Bx1xSxS2_ff0': mask_Bx1xSxS2_ff0, 'mask_Bx1xSxS2_fk0': mask_Bx1xSxS2_fk0, 'L0_xattn_Wq1': _L0_xattn_in['Wq1'], 'L0_xattn_Wk1': _L0_xattn_in['Wk1'], 'L0_xattn_Wv1': _L0_xattn_in['Wv1'], 'L0_xattn_Wq2': _L0_xattn_in['Wq2'], 'L0_xattn_Wk2': _L0_xattn_in['Wk2'], 'L0_xattn_Wv2': _L0_xattn_in['Wv2'], 'L0_xattn_ln1_g': _L0_xattn_in['ln1_g'], 'L0_xattn_ln1_b': _L0_xattn_in['ln1_b'], 'L0_xattn_ln2_g': _L0_xattn_in['ln2_g'], 'L0_xattn_ln2_b': _L0_xattn_in['ln2_b'], 'L0_xattn_ln3_g': _L0_xattn_in['ln3_g'], 'L0_xattn_ln3_b': _L0_xattn_in['ln3_b'], 'L0_xattn_fc1_w': _L0_xattn_in['fc1_w'], 'L0_xattn_fc1_b': _L0_xattn_in['fc1_b'], 'L0_xattn_fc2_w': _L0_xattn_in['fc2_w'], 'L0_xattn_fc2_b': _L0_xattn_in['fc2_b'], 'L1_xattn_ln1_w': _L1_xattn_in['ln1_w'], 'L1_xattn_ln2_w': _L1_xattn_in['ln2_w'], 'L1_xattn_Wq': _L1_xattn_in['Wq'], 'L1_xattn_Wk': _L1_xattn_in['Wk'], 'L1_xattn_Wv': _L1_xattn_in['Wv'], 'L1_xattn_Wo': _L1_xattn_in['Wo'], 'L1_xattn_Wgate': _L1_xattn_in['Wgate'], 'L1_xattn_Wup': _L1_xattn_in['Wup'], 'L1_xattn_Wdown': _L1_xattn_in['Wdown'], 'L2_xattn_Wq': _L2_xattn_in['Wq'], 'L2_xattn_bq': _L2_xattn_in['bq'], 'L2_xattn_Wk': _L2_xattn_in['Wk'], 'L2_xattn_bk': _L2_xattn_in['bk'], 'L2_xattn_Wv': _L2_xattn_in['Wv'], 'L2_xattn_bv': _L2_xattn_in['bv'], 'L2_xattn_Wo': _L2_xattn_in['Wo'], 'L2_xattn_bo': _L2_xattn_in['bo'], 'L2_xattn_gq': _L2_xattn_in['gq'], 'L2_xattn_betaq': _L2_xattn_in['betaq'], 'L2_xattn_gkv': _L2_xattn_in['gkv'], 'L2_xattn_betakv': _L2_xattn_in['betakv'], 'L3_xattn_Wq': _L3_xattn_in['Wq'], 'L3_xattn_bq': _L3_xattn_in['bq'], 'L3_xattn_Wk': _L3_xattn_in['Wk'], 'L3_xattn_bk': _L3_xattn_in['bk'], 'L3_xattn_Wv': _L3_xattn_in['Wv'], 'L3_xattn_bv': _L3_xattn_in['bv'], 'L3_xattn_Wo': _L3_xattn_in['Wo'], 'L3_xattn_bo': _L3_xattn_in['bo'], 'L3_xattn_gamma': _L3_xattn_in['gamma'], 'L3_xattn_beta': _L3_xattn_in['beta']}

def reference(x, ctx_1024, mask_Bx1xSxS2_ff0, mask_Bx1xSxS2_fk0, L0_xattn_Wq1, L0_xattn_Wk1, L0_xattn_Wv1, L0_xattn_Wq2, L0_xattn_Wk2, L0_xattn_Wv2, L0_xattn_ln1_g, L0_xattn_ln1_b, L0_xattn_ln2_g, L0_xattn_ln2_b, L0_xattn_ln3_g, L0_xattn_ln3_b, L0_xattn_fc1_w, L0_xattn_fc1_b, L0_xattn_fc2_w, L0_xattn_fc2_b, L1_xattn_ln1_w, L1_xattn_ln2_w, L1_xattn_Wq, L1_xattn_Wk, L1_xattn_Wv, L1_xattn_Wo, L1_xattn_Wgate, L1_xattn_Wup, L1_xattn_Wdown, L2_xattn_Wq, L2_xattn_bq, L2_xattn_Wk, L2_xattn_bk, L2_xattn_Wv, L2_xattn_bv, L2_xattn_Wo, L2_xattn_bo, L2_xattn_gq, L2_xattn_betaq, L2_xattn_gkv, L2_xattn_betakv, L3_xattn_Wq, L3_xattn_bq, L3_xattn_Wk, L3_xattn_bk, L3_xattn_Wv, L3_xattn_bv, L3_xattn_Wo, L3_xattn_bo, L3_xattn_gamma, L3_xattn_beta):
    import jax
    import jax.numpy as jnp

    def _L0_xattn_ref(x, context, Wq1, Wk1, Wv1, Wq2, Wk2, Wv2, ln1_g, ln1_b, ln2_g, ln2_b, ln3_g, ln3_b, fc1_w, fc1_b, fc2_w, fc2_b):
        import jax, jax.numpy as jnp
        import numpy as np
        EPS = 1e-05

        def _layernorm(x, g, b):
            m = jnp.mean(x, axis=-1, keepdims=True)
            v = jnp.mean((x - m) ** 2, axis=-1, keepdims=True)
            return (x - m) / jnp.sqrt(v + EPS) * g + b

        def _mha(x, kv, Wq, Wk, Wv, mask, causal):
            m = mask[:, None]
            Q = jnp.einsum('bsd,hdk->bhsk', x, Wq) * m
            K = jnp.einsum('bsd,hdk->bhsk', kv, Wk) * m
            V = jnp.einsum('bsd,hdk->bhsk', kv, Wv) * m
            energy = jnp.einsum('bhsk,bhtk->bhst', Q, K)
            S = energy.shape[-1]
            lengths = jnp.sum(energy[:, :, 0, :] != 0, axis=-1)
            cols = jnp.arange(S)
            energy = jnp.where(cols[None, None, None, :] >= lengths[:, :, None, None], -jnp.inf, energy)
            if causal:
                energy = jnp.where(cols[None, :] > cols[:, None], -jnp.inf, energy)
            dk = Wq.shape[-1]
            score = jax.nn.softmax(energy / jnp.sqrt(jnp.asarray(dk, energy.dtype)), axis=-1)
            out = jnp.einsum('bhst,bhtk->bhsk', score, V) * m
            B, H, Sx, dkk = out.shape
            return out.transpose(0, 2, 1, 3).reshape(B, Sx, H * dkk)
        mask0 = 1.0 - jnp.all(x == 0, axis=2, keepdims=True).astype(x.dtype)
        z = _mha(x, x, Wq1, Wk1, Wv1, mask0, causal=True)
        x1 = _layernorm(x + z, ln1_g, ln1_b)
        mask1 = 1.0 - jnp.all(x1 == 0, axis=2, keepdims=True).astype(x1.dtype)
        z = _mha(x1, context, Wq2, Wk2, Wv2, mask1, causal=False)
        x2 = _layernorm(x1 + z, ln2_g, ln2_b)
        z = jnp.maximum(x2 @ fc1_w.T + fc1_b, 0.0) * mask0
        z = (z @ fc2_w.T + fc2_b) * mask0
        return _layernorm(x2 + z, ln3_g, ln3_b)

    def _L1_xattn_ref(hidden_states, kv_states, attention_mask, ln1_w, ln2_w, Wq, Wk, Wv, Wo, Wgate, Wup, Wdown):
        import jax, jax.numpy as jnp
        import numpy as np
        import math
        H, NH, NKV, HD, FF = (256, 16, 4, 64, 1024)
        B, S = (2, 512)
        EPS, THETA = (1e-06, 10000.0)

        def _rmsnorm(x, w, eps=EPS):
            v = jnp.mean(x.astype(jnp.float32) ** 2, axis=-1, keepdims=True)
            return (x.astype(jnp.float32) * jax.lax.rsqrt(v + eps)).astype(x.dtype) * w

        def _rope_tables(seq_len, head_dim, theta=THETA):
            inv_freq = 1.0 / theta ** (jnp.arange(0, head_dim, 2, dtype=jnp.float32) / head_dim)
            freqs = jnp.arange(seq_len, dtype=jnp.float32)[:, None] * inv_freq[None, :]
            emb = jnp.concatenate([freqs, freqs], axis=-1)
            return (jnp.cos(emb), jnp.sin(emb))

        def _rotate_half(x):
            x1, x2 = jnp.split(x, 2, axis=-1)
            return jnp.concatenate([-x2, x1], axis=-1)

        def _apply_rope(x, cos, sin):
            return x * cos[None, None] + _rotate_half(x) * sin[None, None]
        bsz, q_len, _ = hidden_states.shape
        k_len = kv_states.shape[1]
        residual = hidden_states
        h = _rmsnorm(hidden_states, ln1_w)
        kv = _rmsnorm(kv_states, ln1_w)
        q = (h @ Wq).reshape(bsz, q_len, NH, HD).transpose(0, 2, 1, 3)
        k = (kv @ Wk).reshape(bsz, k_len, NKV, HD).transpose(0, 2, 1, 3)
        v = (kv @ Wv).reshape(bsz, k_len, NKV, HD).transpose(0, 2, 1, 3)
        cos_q, sin_q = _rope_tables(q_len, HD)
        cos_k, sin_k = _rope_tables(k_len, HD)
        q = _apply_rope(q, cos_q, sin_q)
        k = _apply_rope(k, cos_k, sin_k)
        groups = NH // NKV
        k = jnp.repeat(k, groups, axis=1)
        v = jnp.repeat(v, groups, axis=1)
        scores = jnp.einsum('bhqd,bhkd->bhqk', q, k) / math.sqrt(HD)
        scores = scores + attention_mask
        probs = jax.nn.softmax(scores.astype(jnp.float32), axis=-1).astype(q.dtype)
        attn = jnp.einsum('bhqk,bhkd->bhqd', probs, v)
        attn = attn.transpose(0, 2, 1, 3).reshape(bsz, q_len, NH * HD)
        attn = attn @ Wo
        hidden = residual + attn
        residual = hidden
        x = _rmsnorm(hidden, ln2_w)
        x = jax.nn.silu(x @ Wgate) * (x @ Wup) @ Wdown
        return residual + x

    def _L2_xattn_ref(query, context, Wq, bq, Wk, bk, Wv, bv, Wo, bo, gq, betaq, gkv, betakv):
        import jax, jax.numpy as jnp
        import numpy as np
        DIM = 256
        N_HEADS = 16
        HEAD_DIM = DIM // N_HEADS
        LN_EPS = 1e-05

        def layer_norm(x, gamma, beta):
            mu = jnp.mean(x, axis=-1, keepdims=True)
            var = jnp.var(x, axis=-1, keepdims=True)
            return (x - mu) * jax.lax.rsqrt(var + LN_EPS) * gamma + beta
        B, Nq, D = query.shape
        Nc = context.shape[1]
        residual = query
        q = layer_norm(query, gq, betaq)
        c = layer_norm(context, gkv, betakv)
        Q = (q @ Wq + bq).reshape(B, Nq, N_HEADS, HEAD_DIM).transpose(0, 2, 1, 3)
        K = (c @ Wk + bk).reshape(B, Nc, N_HEADS, HEAD_DIM).transpose(0, 2, 1, 3)
        V = (c @ Wv + bv).reshape(B, Nc, N_HEADS, HEAD_DIM).transpose(0, 2, 1, 3)
        scores = jnp.einsum('bhqd,bhkd->bhqk', Q, K) / np.sqrt(HEAD_DIM).astype(np.float32)
        attn = jax.nn.softmax(scores, axis=-1)
        out = jnp.einsum('bhqk,bhkd->bhqd', attn, V)
        out = out.transpose(0, 2, 1, 3).reshape(B, Nq, D)
        return residual + out @ Wo + bo

    def _L3_xattn_ref(query, key_in, mask, Wq, bq, Wk, bk, Wv, bv, Wo, bo, gamma, beta):
        import jax, jax.numpy as jnp
        import numpy as np
        ALPHA = 0.5
        SCORES_CLAMP = 50.0
        LN_EPS = 1e-05
        N_HEADS = 16
        B, Qlen, D = query.shape
        Klen = key_in.shape[1]
        H = N_HEADS
        hd = D // H
        q = (query @ Wq + bq).reshape(B, Qlen, H, hd).transpose(0, 2, 1, 3)
        k = (key_in @ Wk + bk).reshape(B, Klen, H, hd).transpose(0, 2, 1, 3)
        v = (key_in @ Wv + bv).reshape(B, Klen, H, hd).transpose(0, 2, 1, 3)
        scores = jnp.einsum('bhqd,bhkd->bhqk', q, k) / jnp.sqrt(jnp.float32(hd))
        scores = ALPHA * (scores * mask) + (1.0 - ALPHA) * scores
        scores = jnp.clip(scores, -SCORES_CLAMP, SCORES_CLAMP)
        attn = jax.nn.softmax(scores, axis=-1)
        context = jnp.einsum('bhqk,bhkd->bhqd', attn, v)
        context = context.transpose(0, 2, 1, 3).reshape(B, Qlen, D)
        out = context @ Wo + bo
        resid = query + out
        mu = jnp.mean(resid, axis=-1, keepdims=True)
        var = jnp.mean(jnp.square(resid - mu), axis=-1, keepdims=True)
        return (resid - mu) * jax.lax.rsqrt(var + LN_EPS) * gamma + beta
    x = _L0_xattn_ref(x, ctx_1024, L0_xattn_Wq1, L0_xattn_Wk1, L0_xattn_Wv1, L0_xattn_Wq2, L0_xattn_Wk2, L0_xattn_Wv2, L0_xattn_ln1_g, L0_xattn_ln1_b, L0_xattn_ln2_g, L0_xattn_ln2_b, L0_xattn_ln3_g, L0_xattn_ln3_b, L0_xattn_fc1_w, L0_xattn_fc1_b, L0_xattn_fc2_w, L0_xattn_fc2_b)
    x = _L1_xattn_ref(x, ctx_1024, mask_Bx1xSxS2_ff0, L1_xattn_ln1_w, L1_xattn_ln2_w, L1_xattn_Wq, L1_xattn_Wk, L1_xattn_Wv, L1_xattn_Wo, L1_xattn_Wgate, L1_xattn_Wup, L1_xattn_Wdown)
    x = _L2_xattn_ref(x, ctx_1024, L2_xattn_Wq, L2_xattn_bq, L2_xattn_Wk, L2_xattn_bk, L2_xattn_Wv, L2_xattn_bv, L2_xattn_Wo, L2_xattn_bo, L2_xattn_gq, L2_xattn_betaq, L2_xattn_gkv, L2_xattn_betakv)
    x = _L3_xattn_ref(x, ctx_1024, mask_Bx1xSxS2_fk0, L3_xattn_Wq, L3_xattn_bq, L3_xattn_Wk, L3_xattn_bk, L3_xattn_Wv, L3_xattn_bv, L3_xattn_Wo, L3_xattn_bo, L3_xattn_gamma, L3_xattn_beta)
    return x

_drawn_inputs = setup_inputs


def setup_inputs(seed=0):
    import zlib

    import numpy as np

    out = dict(_drawn_inputs(seed))
    spreads = {'L0_xattn_ln1_g': (1.0, 0.2),
     'L0_xattn_ln1_b': (0.0, 0.1),
     'L0_xattn_ln2_g': (1.0, 0.2),
     'L0_xattn_ln2_b': (0.0, 0.1),
     'L0_xattn_ln3_g': (1.0, 0.2),
     'L0_xattn_ln3_b': (0.0, 0.1),
     'L0_xattn_fc1_b': (0.0, 0.516),
     'L0_xattn_fc2_b': (0.0, 0.1),
     'L1_xattn_ln1_w': (1.0, 0.6),
     'L1_xattn_ln2_w': (1.0, 0.6),
     'L2_xattn_bq': (0.0, 0.519),
     'L2_xattn_bk': (0.0, 0.8),
     'L2_xattn_bv': (0.0, 0.1),
     'L2_xattn_bo': (0.0, 0.1),
     'L2_xattn_gq': (1.0, 0.2),
     'L2_xattn_betaq': (0.0, 0.517),
     'L2_xattn_gkv': (1.0, 0.2),
     'L2_xattn_betakv': (0.0, 0.1),
     'L3_xattn_bq': (0.0, 0.739),
     'L3_xattn_bk': (0.0, 0.8),
     'L3_xattn_bv': (0.0, 0.1),
     'L3_xattn_bo': (0.0, 0.1),
     'L3_xattn_gamma': (1.0, 0.2),
     'L3_xattn_beta': (0.0, 0.1)}
    factors = {'L0_xattn_Wq1': 8.0,
     'L0_xattn_Wk1': 8.0,
     'L0_xattn_Wq2': 8.0,
     'L0_xattn_Wk2': 8.0,
     'L1_xattn_Wq': 8.0,
     'L1_xattn_Wk': 8.0}
    for name, (base, spread) in spreads.items():
        noise = np.random.default_rng([zlib.crc32(name.encode()), seed]).standard_normal(out[name].shape)
        drawn = base * np.exp(spread * noise) if base else spread * noise
        out[name] = jnp.asarray(drawn.astype(out[name].dtype))
    for name, factor in factors.items():
        out[name] = (out[name] * factor).astype(out[name].dtype)
    return out
```

```python
from contextlib import ExitStack

import numpy as np

import concourse.bass as bass
from concourse import mybir

P = 128
B = 64
S = 128
D = 256
C = D // P
H = 16
G = 4
NG = B // G
U = 4
HU = H // U
FF = 1024
FB = FF // P
NKV = 4
HD = FF // H
VW = 32
VW1 = HD + 2
MASKED = -1.0e30

WEIGHTS = [("qk0", 2 * 512), ("v0", 2 * 256), ("qk1", 2 * 512), ("v1", 2 * 256), ("fc1", 2 * 256), ("fc2", 2 * 256),
           ("q2", 2 * 1024), ("kv2", 2 * 512), ("o2", 8 * 256), ("gate", 2 * 1024), ("up", 2 * 1024),
           ("down", 8 * 256), ("qk3", 2 * 512), ("v3", 2 * 256), ("o3", 2 * 256), ("qk4", 2 * 512), ("v4", 2 * 256),
           ("o4", 2 * 256)]
ROWS = ["ln1g", "ln1b", "ln2g", "ln2b", "ln3g", "ln3b", "fc2b", "bo3", "bo4", "gamma", "beta"]
COLS = ["fc1b", "rms1", "rms2", "bq3", "bk3", "bv3", "gq", "betaq", "gkv", "betakv", "bq4", "bk4", "bv4"]
CONSTS = [("ident", 128), ("causal", 128), ("iota", 128), ("cosq", 64), ("sinq", 64), ("cosk", 64), ("sink", 64),
          ("head8", 8), ("head8q", 8), ("bd", 32), ("expo", 2)]


def offsets(items):
    at, out = 0, {}
    for name, width in items:
        out[name] = (at, width)
        at += width
    return out, at


W_OFF, W_ALL = offsets(WEIGHTS)
R_OFF, R_ALL = offsets([(n, D) for n in ROWS])
K_OFF, K_ALL = offsets([(n, C) for n in COLS])
C_OFF, C_ALL = offsets(CONSTS)


T_LAG, PV_LAG, OUT_LAG = 2, 3, 5


def attention_steps(has_out):
    n_units = G * U
    for n in range(n_units + PV_LAG + (OUT_LAG if has_out else 0)):
        last = n - PV_LAG - OUT_LAG + 3
        yield (n if n < n_units else None,
               n - T_LAG if 0 <= n - T_LAG < n_units else None,
               n - PV_LAG if 0 <= n - PV_LAG < n_units else None,
               last // U if has_out and last >= U - 1 and last % U == U - 1 and last // U < G else None)


def bank_plan():
    plan = []

    def attention(a):
        for _, _, pv, out in attention_steps(a != 2):
            if pv is not None:
                if a == 2:
                    plan.append(("pv2", pv))
                elif pv % U == 0:
                    plan.append((f"pv{a}", pv // U))
            if out is not None:
                plan.append((f"on{a}", out))

    plan += [("xT", b) for b in range(G)]
    for a in range(5):
        if a == 1:
            plan += [("tr1", b) for b in range(G)]
        if a == 3:
            plan += [("tr3", b) for b in range(G)]
        if a == 4:
            for b in range(G):
                plan += [("tr4", b), ("mask4", b)]
        if a == 2:
            plan += [("x2T", b) for b in range(G)]
            for b in range(G + 1):
                plan += [("h", b)] if b < G else []
                plan += [("z", b - 1)] if b else []
            plan += [("tr2", b) for b in range(G)]
            for b in range(G + 1):
                plan += [("q2a", b), ("q2b", b), ("kv2", b)] if b < G else []
                plan += [("qT2a", b - 1), ("qT2b", b - 1), ("kT2", b - 1)] if b else []
        else:
            for b in range(G + 1):
                plan += [(f"m{a}", b), (f"sv{a}", b)] if b < G else []
                if a < 2 and b:
                    plan.append((f"e{a}", b - 1))
        attention(a)
        if a == 2:
            for b in range(G + 1):
                plan += [("aTa", b), ("aTb", b)] if b < G else []
                plan += [("o2", b - 1)] if b else []
            plan += [("nT", b) for b in range(G)]
            for b in range(G + 1):
                plan += [("g0", b), ("u0", b), ("g1", b), ("u1", b)] if b < G else []
                plan += [("dn", b - 1)] if b else []
        if a > 2:
            for b in range(G + 1):
                plan += [(f"zT{a}", b)] if b < G else []
                plan += [(f"o{a}", b - 1)] if b else []
    return plan


N_GEN = 3


def count_plan():
    return {use: (k % N_GEN, k // N_GEN + 1) for k, use in enumerate(bank_plan())}


def build(nc, x_d, ctx_d, mask1_d, mask3_d, w_d, rows_d, cols_d, consts_d, out_d):
    fp32, bf16 = mybir.dt.float32, mybir.dt.bfloat16
    ALU, ACT, AX = mybir.AluOpType, mybir.ActivationFunctionType, mybir.AxisListType
    es = ExitStack()
    with es:
        def sb(name, shape, dt=fp32):
            return es.enter_context(nc.sbuf_tensor(name, shape, dt))

        w_sb = sb("w_sb", [P, W_ALL])
        rows_sb = sb("rows_sb", [P, R_ALL])
        cols_sb = sb("cols_sb", [P, K_ALL])
        consts = sb("consts", [P, C_ALL])
        identb = sb("identb", [P, P], bf16)
        causalb = sb("causalb", [P, P], bf16)
        qbias = sb("qbias", [P, 2, C])
        kbias = sb("kbias", [P, 2, C])
        vbias = sb("vbias", [P, 2, C])
        xs = sb("xs", [P, G, D])
        ctx = sb("ctx", [P, G, D])
        ctx_ln = sb("ctx_ln", [P, G, D])
        ctx_rms = sb("ctx_rms", [P, G, D])
        res = sb("res", [P, G, D])
        zn = sb("zn", [P, G, D])
        actT = sb("actT", [P, G, 4, P])
        plainT = sb("plainT", [P, G, C, P])
        v16 = sb("v16", [P, G, H, VW])
        v64 = sb("v64", [P, G, NKV, VW1])
        wide = sb("wide", [P, G, 2 * FF])
        oT = sb("oT", [P, 2, U, S])
        mask1 = sb("mask1", [P, G, S])
        mask3 = sb("mask3", [P, G, S])
        fT = sb("fT", [P, G, S])
        nat = wide[:, :, 0:FF]
        tr = wide[:, :, FF:2 * FF].rearrange("p g (c s) -> p g c s", s=P)
        by_head_T = wide[:, :, :].rearrange("p g (h s) -> p g h s", h=H)
        ctx_m = res
        outn = res
        keyT = zn[:, :, :].rearrange("p g (c s) -> p g c s", c=C)
        prob = sb("prob", [P, 4, HU, S])
        probT = sb("probT", [P, 4, HU, S])
        masked = sb("masked", [P, 3, HU, S])
        ropes = prob[:, :, :, :].rearrange("p n h s -> p n (h s)")
        negmax = sb("negmax", [P, 4, HU])
        posmax = sb("posmax", [P, 4, HU])
        absmax = sb("absmax", [P, G])
        live = sb("live", [P, 2, G])
        st = sb("st", [P, G, 6])
        mv = sb("mv", [P, G, 2])
        ve = sb("ve", [P, G, 2])
        rstd = sb("rstd", [P, G, 2])
        cst = sb("cst", [P, G, 6])
        cmv = sb("cmv", [P, G, 2])
        cve = sb("cve", [P, G, 2])
        crstd = sb("crstd", [P, G, 2])
        ssq = sb("ssq", [P, G])
        rden = sb("rden", [P, G, H])
        rdenm = sb("rdenm", [P, G, H])
        q0 = sb("q0", [P, G, C, H])
        nz = sb("nz", [H, G, S])
        count = sb("count", [H, G])
        fill = sb("fill", [H, G, 2])
        pen = sb("pen", [P, G, S], bf16)
        scores_ps = es.enter_context(nc.psum_tensor("scores_ps", [P, 3, 512], fp32))
        probT_ps = es.enter_context(nc.psum_tensor("probT_ps", [P, 2, 512], fp32))
        gen_ps = es.enter_context(nc.psum_tensor("gen_ps", [P, N_GEN, 512], fp32))

        names = {}

        def sem(name):
            if name not in names:
                names[name] = es.enter_context(nc.semaphore(name))
            return names[name]

        bank_full = [sem(f"bank_full{j}") for j in range(N_GEN)]
        bank_read = [sem(f"bank_read{j}") for j in range(N_GEN)]
        plan = count_plan()

        def W(name):
            at, width = W_OFF[name]
            k = {"o2": 8, "down": 8}.get(name, 2)
            return w_sb[:, at:at + width].rearrange("p (c n) -> p c n", c=k)

        def row(name):
            at, width = R_OFF[name]
            return rows_sb[:, at:at + width]

        def col(name, c):
            at, _ = K_OFF[name]
            return cols_sb[:, at + c:at + c + 1]

        def const(name):
            at, width = C_OFF[name]
            return consts[:, at:at + width]

        ident = const("ident")

        def bank(name, i):
            return gen_ps[:, plan[name, i][0], :]

        def take(eng, name, i):
            j, use = plan[name, i]
            eng.wait_ge(bank_full[j], use)
            return gen_ps[:, j, :]

        def release(ins, name, i):
            ins.then_inc(bank_read[plan[name, i][0]], 1)

        def read_out(eng, name, i):
            j, use = plan[name, i]
            eng.wait_ge(bank_read[j], use)

        def values_done(eng, N):
            a, n = N // (G * U), N % (G * U)
            b, u = n // U, n % U
            if a == 2 or u == U - 1:
                j, use = plan[("pv2", n) if a == 2 else (f"pv{a}", b)]
                eng.wait_ge(bank_full[j], use)
            else:
                eng.wait_ge(sem("values_done"), ((a - (a > 2)) * G + b) * (U - 1) + u + 1)

        with nc.Block() as block:
            @block.sync
            def _(sp):
                sp.dma_start(consts[:, :], consts_d).then_inc(sem("su_cols"), 16)
                sp.dma_start(cols_sb[:, :], cols_d).then_inc(sem("su_cols"), 16)
                sp.dma_start(rows_sb[:, :], rows_d).then_inc(sem("su_rows"), 16)
                half = W_OFF["q2"][0]
                sp.dma_start(w_sb[:, half:W_ALL], w_d[:, half:W_ALL]).then_inc(sem("su_w"), 16)
                sp.dma_start(w_sb[:, 0:half], w_d[:, 0:half]).then_inc(sem("su_w0"), 16)
                sp.wait_ge(sem("su_w0"), 16)

            @block.gpsimd
            def _(pool):
                pool.memset(v16[:, :, :, :], 0.0).then_inc(sem("su_v"), 1)
                pool.memset(v64[:, :, :, :], 0.0).then_inc(sem("su_v"), 1)
                pool.wait_ge(sem("su_v"), 2)
                pool.memset(v16[:, :, :, 16:17], 1.0).then_inc(sem("su_v"), 1)
                pool.memset(v64[:, :, :, HD:HD + 1], 1.0).then_inc(sem("su_v"), 1)
                pool.memset(pen[:, :, :], 0.0).then_inc(sem("su_v"), 1)
                pool.wait_ge(sem("su_v"), 5)

            @block.tensor
            def _(pe):
                pe.wait_ge(sem("su_w"), 16)
                pe.wait_ge(sem("su_cols"), 32)
                for k, (w, first, beta) in enumerate([("qk3", 0, "betaq"), ("qk3", 256, "betakv"), ("v3", 0, "betakv")]):
                    for n in range(C):
                        for c in range(C):
                            last = nc.tensor.matmul(gen_ps[:, 0, 2 * k + n:2 * k + n + 1],
                                                    W(w)[:, c, first + n * P:first + (n + 1) * P], col(beta, c),
                                                    start=(c == 0), stop=(c == C - 1))
                last.then_inc(sem("su_beta"), 1)
                pe.wait_ge(sem("su_vb"), 1)
                for a in range(2):
                    for c in range(C):
                        last = nc.tensor.matmul(gen_ps[:, 1, a * D:(a + 1) * D], masked[:, c, 0, :]
                                                if a == 0 else probT[:, c, 0, :], W(f"o{3 + a}")[:, c, :],
                                                start=(c == 0), stop=(c == C - 1))
                last.then_inc(sem("su_bo"), 1)

            @block.vector
            def _(dve):
                dve.wait_ge(sem("su_cols"), 32)
                nc.vector.tensor_copy(identb[:, :], ident)
                nc.vector.tensor_copy(causalb[:, :], const("causal"))
                dve.wait_ge(sem("su_beta"), 1)
                own = [0]

                def step(ins):
                    own[0] += 1
                    ins.then_inc(sem("su_dve"), 1)

                for c in range(C):
                    step(nc.vector.tensor_tensor(vbias[:, 0, c:c + 1], gen_ps[:, 0, 4 + c:5 + c], col("bv3", c), ALU.add))
                    step(nc.vector.tensor_copy(vbias[:, 1, c:c + 1], col("bv4", c)))
                    step(nc.vector.tensor_tensor(kbias[:, 0, c:c + 1], gen_ps[:, 0, 2 + c:3 + c], col("bk3", c), ALU.add))
                    step(nc.vector.tensor_copy(kbias[:, 1, c:c + 1], col("bk4", c)))
                    step(nc.vector.tensor_tensor(qbias[:, 0, c:c + 1], gen_ps[:, 0, c:c + 1], col("bq3", c), ALU.add))
                    step(nc.vector.tensor_copy(qbias[:, 1, c:c + 1], col("bq4", c)))
                dve.wait_ge(sem("su_dve"), own[0])
                step(nc.vector.tensor_scalar(qbias[:, 0, :], qbias[:, 0, :], 0.25, None, ALU.mult))
                for a in range(2):
                    for c in range(C):
                        dst = masked[:, c, 0, :] if a == 0 else probT[:, c, 0, :]
                        step(nc.vector.tensor_copy(dst, vbias[:, a, c:c + 1].to_broadcast([P, P])))
                dve.wait_ge(sem("su_dve"), own[0])
                nc.vector.nop().then_inc(sem("su_vb"), 1)
                for w, g in [("q2", "rms1"), ("kv2", "rms1"), ("gate", "rms2"), ("up", "rms2")]:
                    for c in range(C):
                        nc.vector.tensor_scalar(W(w)[:, c, :], W(w)[:, c, :], col(g, c), None, ALU.mult)
                for w, first, g in [("qk3", 0, "gq"), ("qk3", 256, "gkv"), ("v3", 0, "gkv")]:
                    for c in range(C):
                        nc.vector.tensor_scalar(W(w)[:, c, first:first + D], W(w)[:, c, first:first + D], col(g, c),
                                                None, ALU.mult)
                dve.wait_ge(sem("su_rows"), 16)
                dve.wait_ge(sem("su_bo"), 1)
                for a in range(2):
                    ins = nc.vector.tensor_tensor(row(f"bo{3 + a}"), gen_ps[:, 1, a * D:(a + 1) * D],
                                                  row(f"bo{3 + a}"), ALU.add)
                ins.then_inc(sem("su_end"), 1)
                dve.wait_ge(sem("su_end"), 1)

        x_g = x_d.rearrange("(n g) s d -> n s g d", g=G)
        ctx_g = ctx_d.rearrange("(n g) s d -> n s g d", g=G)
        mask1_g = mask1_d.rearrange("(n g) a s t -> n s g (a t)", g=G)
        mask3_g = mask3_d.rearrange("(n g) a s t -> n s g (a t)", g=G)
        out_g = out_d.rearrange("(n g) s d -> n s g d", g=G)

        setup_names = set(names)
        with nc.Fori(0, NG) as i:
            with nc.Block() as block:
                @block.sync
                def _(sp):
                    sp.dma_start(xs[:, :, :], x_g[i]).then_inc(sem("x_in"), 16)
                    sp.dma_start(ctx[:, :, :], ctx_g[i]).then_inc(sem("ctx_in"), 16)
                    sp.dma_start(mask1[:, :, :], mask1_g[i]).then_inc(sem("mask1_in"), 16)
                    sp.dma_start(mask3[:, :, :], mask3_g[i]).then_inc(sem("mask3_in"), 16)
                    for b in range(G):
                        sp.wait_ge(sem("out_ready"), b + 1)
                        sp.dma_start(out_g[i][:, b, :], outn[:, b, :]).then_inc(sem("stored"), 16)
                    sp.wait_ge(sem("stored"), 16 * G)

                @block.tensor
                def _(pe):
                    def begin(name, i_):
                        j, use = plan[name, i_]
                        if use > 1:
                            pe.wait_ge(bank_read[j], use - 1)
                        return gen_ps[:, j, :]

                    def end(ins, name, i_):
                        ins.then_inc(bank_full[plan[name, i_][0]], 1)

                    def transposes(name, b, sources):
                        ps = begin(name, b)
                        for k, src in enumerate(sources):
                            last = nc.tensor.transpose(ps[:, k * P:(k + 1) * P], src, ident)
                        end(last, name, b)

                    def halves(t):
                        return [t[:, c * P:(c + 1) * P] for c in range(C)]

                    def product(ps, lhsT, rhs, chunks):
                        for c in range(chunks):
                            last = nc.tensor.matmul(ps, lhsT(c), rhs(c), start=(c == 0), stop=(c == chunks - 1))
                        return last

                    def qkv(a, b):
                        kv = 0 if a == 0 else 2
                        key_first, query_first = (D, kv), (0, 0)
                        moving, plain = (query_first, key_first) if a == 4 else (key_first, query_first)
                        for name, (first, src) in [(f"m{a}", moving), (f"sv{a}", plain)]:
                            ps = begin(name, b)
                            for n in range(C):
                                last = product(ps[:, n * P:(n + 1) * P],
                                               lambda c: W(f"qk{a}")[:, c, first + n * P:first + (n + 1) * P],
                                               lambda c: actT[:, b, src + c, :], C)
                            if name[0] == "s":
                                last = product(ps[:, D:2 * D], lambda c: actT[:, b, kv + c, :],
                                               lambda c: W(f"v{a}")[:, c, :], C)
                            end(last, name, b)

                    def first_row(a, b):
                        pe.wait_ge(sem(f"q0_{a}"), b + 1)
                        ps = begin(f"e{a}", b)
                        end(product(ps[0:H, 0:S], lambda c: q0[:, b, c, :], lambda c: keyT[:, b, c, :], C),
                            f"e{a}", b)

                    def scores(a, n):
                        N = a * G * U + n
                        b, u = n // U, n % U
                        ps = scores_ps[:, N % 3, :]
                        if u == 0:
                            for name in ["qT2a", "qT2b", "kT2"] if a == 2 else [f"m{a}", f"sv{a}"]:
                                read_out(pe, name, b)
                            if a < 2:
                                pe.wait_ge(sem(f"pen_{a}"), b + 1)
                        if N >= 3:
                            pe.wait_ge(sem("exp_done"), N - 2)
                        if a == 2:
                            r = (u % 2) * HD
                            for k in range(HU):
                                last = nc.tensor.matmul(ps[:, k * S:(k + 1) * S],
                                                        tr[r:r + HD, b, (u // 2) * HU + k, :],
                                                        plainT[r:r + HD, b, u // 2, :], start=True, stop=True)
                        else:
                            if a == 0:
                                nc.tensor.matmul(ps, identb[:, :],
                                                 causalb[:, :].unsqueeze(1).to_broadcast([P, HU, S]),
                                                 start=True, stop=False, skip_group_check=True)
                            for k in range(HU if a < 2 else 0):
                                h = HU * u + k
                                nc.tensor.matmul(ps[:, k * S:(k + 1) * S], identb[:, h:h + 1].to_broadcast([P, P]),
                                                 pen[:, b, :], start=(a == 1 and k == 0), stop=False,
                                                 skip_group_check=True)
                            last = nc.tensor.matmul(ps, plainT[:, b, u // 2, :],
                                                    by_head_T[:, b, HU * u:HU * (u + 1), :]
                                                    .rearrange("p h s -> p (h s)"), start=(a > 2), stop=True,
                                                    skip_group_check=(a < 2))
                        last.then_inc(sem("scores_full"), 1)

                    def prob_transposes(a, n):
                        N = a * G * U + n
                        pe.wait_ge(sem("exp_done"), N + 1)
                        if N >= 2:
                            pe.wait_ge(sem(f"probT_ready{N % 2}"), N // 2)
                        for k in range(HU):
                            last = nc.tensor.transpose(probT_ps[:, N % 2, k * S:(k + 1) * S], prob[:, N % 4, k, :],
                                                       ident)
                        last.then_inc(sem("probT_full"), 1)

                    def values(a, n):
                        N = a * G * U + n
                        b, u = n // U, n % U
                        if a == 4:
                            pe.wait_ge(sem("exp_done"), N + 1)
                        else:
                            pe.wait_ge(sem(f"probT_ready{N % 2}"), N // 2 + 1)
                        if a == 2:
                            ps = begin("pv2", n)
                            for k in range(HU):
                                last = nc.tensor.matmul(ps[:, k * VW1:(k + 1) * VW1], probT[:, N % 4, k, :],
                                                        v64[:, b, u, :], start=True, stop=True)
                            end(last, "pv2", n)
                            return
                        ps = begin(f"pv{a}", b) if u == 0 else bank(f"pv{a}", b)
                        for k in range(HU):
                            last = nc.tensor.matmul(ps[32 * k:32 * k + 32, u * S:(u + 1) * S],
                                                    v16[:, b, HU * u + k, :], probT[:, N % 4, k, :],
                                                    start=True, stop=True)
                        if u == U - 1:
                            end(last, f"pv{a}", b)
                        else:
                            last.then_inc(sem("values_done"), 1)

                    def attention(a):
                        for s_n, t_n, v_n, o_b in attention_steps(a != 2):
                            if s_n is not None:
                                scores(a, s_n)
                            if t_n is not None and a != 4:
                                prob_transposes(a, t_n)
                            if v_n is not None:
                                values(a, v_n)
                            if o_b is not None:
                                read_out(pe, f"pv{a}", o_b)
                                transposes(f"on{a}", o_b, [oT[:, o_b % 2, u, :] for u in range(U)])

                    pe.wait_ge(sem("x_in"), 16)
                    for b in range(G):
                        transposes("xT", b, halves(xs[:, b, :]))
                    for b in range(G + 1):
                        if b < G:
                            read_out(pe, "xT", b)
                            qkv(0, b)
                        if b:
                            first_row(0, b - 1)
                    attention(0)
                    for b in range(G):
                        pe.wait_ge(sem("x1"), b + 1)
                        pe.wait_ge(sem("ctx_m"), b + 1)
                        transposes("tr1", b, halves(xs[:, b, :]) + halves(ctx_m[:, b, :]))
                    for b in range(G + 1):
                        if b < G:
                            read_out(pe, "tr1", b)
                            qkv(1, b)
                        if b:
                            first_row(1, b - 1)
                    attention(1)
                    for b in range(G):
                        pe.wait_ge(sem("x2"), b + 1)
                        transposes("x2T", b, halves(xs[:, b, :]))
                    for b in range(G + 1):
                        if b < G:
                            read_out(pe, "x2T", b)
                            ps = begin("h", b)
                            for n in range(C):
                                last = product(ps[:, n * P:(n + 1) * P],
                                               lambda c: W("fc1")[:, c, n * P:(n + 1) * P],
                                               lambda c: actT[:, b, c, :], C)
                            end(last, "h", b)
                        if b:
                            read_out(pe, "h", b - 1)
                            ps = begin("z", b - 1)
                            end(product(ps[:, 0:D], lambda c: actT[:, b - 1, 2 + c, :], lambda c: W("fc2")[:, c, :], C),
                                "z", b - 1)
                    for b in range(G):
                        pe.wait_ge(sem("n3"), b + 1)
                        pe.wait_ge(sem("ctx_rms"), b + 1)
                        transposes("tr2", b, halves(zn[:, b, :]) + halves(ctx_rms[:, b, :]))
                    for b in range(G + 1):
                        if b < G:
                            read_out(pe, "tr2", b)
                            for k, name in enumerate(["q2a", "q2b"]):
                                ps = begin(name, b)
                                end(product(ps, lambda c: actT[:, b, c, :],
                                            lambda c: W("q2")[:, c, k * 512:(k + 1) * 512], C), name, b)
                            ps = begin("kv2", b)
                            end(product(ps, lambda c: actT[:, b, 2 + c, :], lambda c: W("kv2")[:, c, :], C), "kv2", b)
                        if b:
                            for k, name in enumerate(["qT2a", "qT2b"]):
                                pe.wait_ge(sem("roped"), 3 * (b - 1) + k + 1)
                                transposes(name, b - 1,
                                           [nat[:, b - 1, (4 * k + m) * P:(4 * k + m + 1) * P] for m in range(4)])
                            pe.wait_ge(sem("roped"), 3 * b)
                            transposes("kT2", b - 1, halves(res[:, b - 1, :]))
                    for s_n, t_n, v_n, _ in attention_steps(False):
                        if s_n is not None:
                            scores(2, s_n)
                        if t_n is not None:
                            prob_transposes(2, t_n)
                        if v_n is not None:
                            values(2, v_n)
                    for b in range(G + 1):
                        if b < G:
                            for k, name in enumerate(["aTa", "aTb"]):
                                read_out(pe, "pv2", U * b + 2 * k)
                                read_out(pe, "pv2", U * b + 2 * k + 1)
                                transposes(name, b,
                                           [nat[:, b, (4 * k + m) * P:(4 * k + m + 1) * P] for m in range(4)])
                        if b:
                            read_out(pe, "aTa", b - 1)
                            read_out(pe, "aTb", b - 1)
                            ps = begin("o2", b - 1)
                            end(product(ps[:, 0:D], lambda c: tr[:, b - 1, c, :], lambda c: W("o2")[:, c, :], FB),
                                "o2", b - 1)
                    for b in range(G):
                        pe.wait_ge(sem("n_h"), b + 1)
                        transposes("nT", b, halves(zn[:, b, :]))
                    for b in range(G + 1):
                        if b < G:
                            read_out(pe, "nT", b)
                            for k in range(2):
                                for name, w in [(f"g{k}", "gate"), (f"u{k}", "up")]:
                                    ps = begin(name, b)
                                    for m in range(4):
                                        f = (4 * k + m) * P
                                        last = product(ps[:, m * P:(m + 1) * P], lambda c: W(w)[:, c, f:f + P],
                                                       lambda c: actT[:, b, c, :], C)
                                    end(last, name, b)
                        if b:
                            read_out(pe, "u0", b - 1)
                            read_out(pe, "u1", b - 1)
                            ps = begin("dn", b - 1)
                            end(product(ps[:, 0:D], lambda c: tr[:, b - 1, c, :], lambda c: W("down")[:, c, :], FB),
                                "dn", b - 1)
                    for b in range(G):
                        pe.wait_ge(sem("n4"), b + 1)
                        pe.wait_ge(sem("ctx_ln"), b + 1)
                        transposes("tr3", b, halves(zn[:, b, :]) + halves(ctx_ln[:, b, :]))
                    for b in range(G):
                        read_out(pe, "tr3", b)
                        qkv(3, b)
                    attention(3)

                    def output(a):
                        for b in range(G + 1):
                            if b < G:
                                read_out(pe, f"on{a}", b)
                                transposes(f"zT{a}", b, halves(zn[:, b, :]))
                            if b:
                                read_out(pe, f"zT{a}", b - 1)
                                ps = begin(f"o{a}", b - 1)
                                end(product(ps[:, 0:D], lambda c: actT[:, b - 1, c, :],
                                            lambda c: W(f"o{a}")[:, c, :], C), f"o{a}", b - 1)

                    output(3)
                    pe.wait_ge(sem("mask3_in"), 16)
                    for b in range(G):
                        read_out(pe, "o3", b)
                        transposes("tr4", b, halves(xs[:, b, :]) + halves(ctx[:, b, :]))
                        transposes("mask4", b, [mask3[:, b, :]])
                    for b in range(G):
                        read_out(pe, "tr4", b)
                        qkv(4, b)
                    attention(4)
                    output(4)

                @block.scalar
                def _(act):
                    def copy_out(name, b, dst, width):
                        release(nc.scalar.activation(dst, take(act, name, b)[:, 0:width], ACT.Copy), name, b)

                    def plain_out(a, b):
                        ps = take(act, f"sv{a}", b)
                        if a < 2:
                            nc.scalar.activation(plainT[:, b, :, :].rearrange("p c s -> p (c s)"), ps[:, 0:D],
                                                 ACT.Copy, scale=0.25)
                        else:
                            for c in range(C):
                                bias, scale = (qbias[:, 0, c:c + 1], 0.25) if a == 3 else (kbias[:, 1, c:c + 1], 1.0)
                                nc.scalar.activation(plainT[:, b, c, :], ps[:, c * P:(c + 1) * P], ACT.Identity,
                                                     bias=bias, scale=scale)
                        release(nc.scalar.activation(v16[:, b, :, 0:16],
                                                     ps[:, D:2 * D].rearrange("p (h d) -> p h d", h=H), ACT.Copy),
                                f"sv{a}", b)

                    def attention(a):
                        for s_n, t_n, v_n, o_b in attention_steps(a != 2):
                            if s_n is not None:
                                N = a * G * U + s_n
                                if a == 4:
                                    act.wait_ge(sem("clipped"), s_n + 1)
                                    values_done(act, N - 4)
                                    nc.scalar.activation(probT[:, N % 4, :, :], masked[:, N % 3, :, :],
                                                         ACT.Exp).then_inc(sem("exp_done"), 1)
                                else:
                                    act.wait_ge(sem("max_done"), N + 1)
                                    if N >= 4:
                                        act.wait_ge(sem("probT_full"), N - 3)
                                    src = masked[:, N % 3, :, :] if a == 2 else \
                                        scores_ps[:, N % 3, :].rearrange("p (k t) -> p k t", k=HU)
                                    for k in range(HU):
                                        ins = nc.scalar.activation(prob[:, N % 4, k, :], src[:, k, :], ACT.Exp,
                                                                   bias=negmax[:, N % 4, k:k + 1])
                                    ins.then_inc(sem("exp_done"), 1)
                            if t_n is not None and a != 4 and (a * G * U + t_n) % 2 == 1:
                                N = a * G * U + t_n
                                act.wait_ge(sem("probT_full"), N + 1)
                                if N >= 4:
                                    values_done(act, N - 4)
                                nc.scalar.activation(probT[:, N % 4, :, :].rearrange("p k s -> p (k s)"),
                                                     probT_ps[:, N % 2, :], ACT.Copy).then_inc(sem("probT_ready1"), 1)
                            if v_n is not None and a != 2 and v_n % U == U - 1:
                                b = v_n // U
                                values_done(act, a * G * U + v_n)
                                release(nc.scalar.activation(oT[:, b % 2, :, :].rearrange("p u s -> p (u s)"),
                                                             bank(f"pv{a}", b), ACT.Copy), f"pv{a}", b)

                    def flat(t):
                        return t.rearrange("p c s -> p (c s)")

                    for b in range(G):
                        copy_out("xT", b, flat(actT[:, b, 0:2, :]), D)
                    for b in range(G):
                        plain_out(0, b)
                    attention(0)
                    for b in range(G):
                        copy_out("tr1", b, flat(actT[:, b, :, :]), 512)
                    for b in range(G):
                        plain_out(1, b)
                    attention(1)
                    for b in range(G):
                        copy_out("x2T", b, flat(actT[:, b, 0:2, :]), D)
                    for b in range(G):
                        ps = take(act, "h", b)
                        for c in range(C):
                            ins = nc.scalar.activation(actT[:, b, 2 + c, :], ps[:, c * P:(c + 1) * P], ACT.Relu,
                                                       bias=col("fc1b", c))
                        release(ins, "h", b)
                    for b in range(G):
                        act.wait_ge(sem("x3"), b + 1)
                        nc.scalar.activation(res[:, b, :], xs[:, b, :], ACT.Square, accum_out=ssq[:, b:b + 1])\
                            .then_inc(sem("ssq3"), 1)
                    for b in range(G):
                        copy_out("tr2", b, flat(actT[:, b, :, :]), 512)
                    for b in range(G):
                        copy_out("qT2a", b, flat(tr[:, b, 0:4, :]), 512)
                        copy_out("qT2b", b, flat(tr[:, b, 4:8, :]), 512)
                    attention(2)
                    for b in range(G):
                        copy_out("aTa", b, flat(tr[:, b, 0:4, :]), 512)
                    for b in range(G):
                        read_out(act, "o2", b)
                        nc.scalar.activation(res[:, b, :], xs[:, b, :], ACT.Square, accum_out=ssq[:, b:b + 1])\
                            .then_inc(sem("ssqh"), 1)
                    for b in range(G):
                        copy_out("nT", b, flat(actT[:, b, 0:2, :]), D)
                    for b in range(G):
                        for k in range(2):
                            ps = take(act, f"g{k}", b)
                            if b:
                                read_out(act, f"g{k}", b - 1)
                            nc.scalar.activation(prob[:, k, :, :].rearrange("p k s -> p (k s)"), ps, ACT.Tanh,
                                                 scale=0.5).then_inc(sem("tanh"), 1)
                    for b in range(G):
                        copy_out("tr3", b, flat(actT[:, b, :, :]), 512)
                    for b in range(G):
                        plain_out(3, b)
                    attention(3)
                    for b in range(G):
                        copy_out("zT3", b, flat(actT[:, b, 0:2, :]), D)
                    for b in range(G):
                        copy_out("tr4", b, flat(actT[:, b, :, :]), 512)
                    for b in range(G):
                        plain_out(4, b)
                    attention(4)
                    for b in range(G):
                        copy_out("zT4", b, flat(actT[:, b, 0:2, :]), D)

                @block.gpsimd
                def _(pool):
                    def rsqrt(src, dst, wait, signal, b, width=1):
                        pool.wait_ge(sem(wait), b + 1)
                        nc.gpsimd.tensor_tensor(dst, src, const("expo")[:, 0:width], ALU.pow)\
                            .then_inc(sem(signal), 1)

                    def add_residual(a, b):
                        read_out(pool, f"on{a}", b)
                        nc.gpsimd.tensor_tensor(res[:, b, :], zn[:, b, :], xs[:, b, :], ALU.add)\
                            .then_inc(sem(f"res_{a}"), 1)

                    for b in range(G):
                        rsqrt(cve[:, b, :], crstd[:, b, :], "cve", "crstd", b, 2)
                        pool.wait_ge(sem("crstd"), b + 1)
                        nc.gpsimd.tensor_scalar(ctx_ln[:, b, :], ctx[:, b, :], cmv[:, b, 0:1], crstd[:, b, 0:1],
                                                ALU.subtract, ALU.mult).then_inc(sem("ctx_ln"), 1)
                        nc.gpsimd.tensor_scalar(ctx_rms[:, b, :], ctx[:, b, :], crstd[:, b, 1:2], 0.0,
                                                ALU.mult, ALU.add).then_inc(sem("ctx_rms"), 1)
                    for a in range(2):
                        for b in range(G):
                            add_residual(a, b)
                            rsqrt(ve[:, b, 0:1], rstd[:, b, 0:1], f"ve_{a}", f"rstd_{a}", b)
                            if a == 0:
                                pool.wait_ge(sem("live1"), b + 1)
                                nc.gpsimd.tensor_scalar(ctx_m[:, b, :], ctx[:, b, :], live[:, 1, b:b + 1], 0.0,
                                                        ALU.mult, ALU.add).then_inc(sem("ctx_m"), 1)
                    for b in range(G):
                        rsqrt(ve[:, b, 0:1], rstd[:, b, 0:1], "ve_m", "rstd_m", b)
                    for b in range(G):
                        rsqrt(ve[:, b, 0:1], rstd[:, b, 0:1], "ve_2", "rstd_2", b)
                    for b in range(G):
                        for k in range(3):
                            m = 3 * b + k
                            read_out(pool, ["q2a", "q2b", "kv2"][k], b)
                            dst = nat[:, b, k * 512:(k + 1) * 512] if k < 2 else res[:, b, :]
                            w = 512 if k < 2 else 256
                            nc.gpsimd.tensor_tensor(dst, ropes[:, m % 2, 0:w], ropes[:, 2 + m % 2, 0:w], ALU.add)\
                                .then_inc(sem("roped"), 1)
                    for b in range(G):
                        rsqrt(ve[:, b, 0:1], rstd[:, b, 0:1], "ve_h", "rstd_h", b)
                    for b in range(G):
                        rsqrt(ve[:, b, 0:1], rstd[:, b, 0:1], "ve_4", "rstd_4", b)
                        nc.gpsimd.tensor_tensor(res[:, b, :], xs[:, b, :], row("bo3"), ALU.add)\
                            .then_inc(sem("res_3"), 1)
                    for b in range(G):
                        read_out(pool, "o3", b)
                        nc.gpsimd.tensor_tensor(res[:, b, :], xs[:, b, :], row("bo4"), ALU.add)\
                            .then_inc(sem("res_4"), 1)
                    for b in range(G):
                        rsqrt(ve[:, b, 0:1], rstd[:, b, 0:1], "ve_5", "rstd_5", b)

                @block.vector
                def _(dve):
                    own = [0]

                    def link(ins):
                        own[0] += 1
                        ins.then_inc(sem("dve_own"), 1)
                        dve.wait_ge(sem("dve_own"), own[0])

                    def nonzero_rows(src, which, b):
                        link(nc.vector.tensor_reduce(absmax[:, b:b + 1], src, AX.X, ALU.max,
                                                     apply_absolute_value=True))
                        return nc.vector.tensor_scalar(live[:, which, b:b + 1], absmax[:, b:b + 1], 0.0, None,
                                                       ALU.is_gt)

                    def per_head(a, b):
                        ps = take(dve, f"m{a}", b)
                        own_rows = const("head8q" if a == 4 else "head8").unsqueeze(2).to_broadcast([P, 8, S])
                        for c in range(C):
                            src = ps[:, c * P:(c + 1) * P].unsqueeze(1).to_broadcast([P, 8, S])
                            dst = by_head_T[:, b, 8 * c:8 * c + 8, :]
                            if a < 2:
                                nc.vector.tensor_tensor(dst, src, own_rows, ALU.mult)
                            else:
                                bias = kbias[:, 0, c:c + 1] if a == 3 else qbias[:, 1, c:c + 1]
                                ins = nc.vector.scalar_tensor_tensor(dst, src, bias, own_rows, ALU.add, ALU.mult)
                        if a < 2:
                            ins = nc.vector.tensor_copy(zn[:, b, :], ps[:, 0:D])
                        release(ins, f"m{a}", b)

                    def first_query(a, b):
                        read_out(dve, f"sv{a}", b)
                        nc.vector.tensor_tensor(q0[:, b, :, :], const("bd").rearrange("p (c h) -> p c h", c=C),
                                                plainT[:, b, :, 0:1].to_broadcast([P, C, H]), ALU.mult)\
                            .then_inc(sem(f"q0_{a}"), 1)

                    def length_penalty(a, b):
                        ps = take(dve, f"e{a}", b)
                        ins = nc.vector.tensor_scalar(nz[:, b, :], ps[0:H, 0:S], 0.0, None, ALU.not_equal)
                        release(ins, f"e{a}", b)
                        read_out(dve, f"e{a}", b)
                        link(nc.vector.tensor_reduce(count[:, b:b + 1], nz[:, b, :], AX.X, ALU.add))
                        link(nc.vector.tensor_scalar(fill[:, b, 0:1], count[:, b:b + 1], 0.5, -3.0e38, ALU.is_lt,
                                                     ALU.mult))
                        link(nc.vector.tensor_scalar(fill[:, b, 1:2], fill[:, b, 0:1], 1.0e10, MASKED, ALU.mult,
                                                     ALU.add))
                        nc.vector.tensor_scalar(pen[0:H, b, :], const("iota")[0:H, :], count[:, b:b + 1],
                                                fill[:, b, 1:2], ALU.is_ge, ALU.mult).then_inc(sem(f"pen_{a}"), 1)

                    def normalized(a, b, which=None):
                        ps = take(dve, f"on{a}", b).rearrange("p (h w) -> p h w", h=H)
                        link(nc.vector.reciprocal(rden[:, b, :], ps[:, :, 16]))
                        rec = rden
                        if which is not None:
                            link(nc.vector.tensor_scalar(rdenm[:, b, :], rden[:, b, :], live[:, which, b:b + 1], None,
                                                         ALU.mult))
                            rec = rdenm
                        ins = nc.vector.tensor_tensor(zn[:, b, :].rearrange("p (h d) -> p h d", h=H), ps[:, :, 0:16],
                                                      rec[:, b, :].unsqueeze(2).to_broadcast([P, H, 16]), ALU.mult)
                        release(ins, f"on{a}", b)

                    def statistics(src, b, eps, signal):
                        link(nc.vector.bn_stats(st[:, b, :], src))
                        link(nc.vector.bn_aggr(mv[:, b, :], st[:, b, :]))
                        nc.vector.tensor_scalar(ve[:, b, 0:1], mv[:, b, 1:2], eps, None, ALU.add)\
                            .then_inc(sem(signal), 1)

                    def layernorm(src, dst, gain, bias, b, rstd_ready, signal):
                        link(nc.vector.scalar_tensor_tensor(zn[:, b, :], src, mv[:, b, 0:1], row(gain), ALU.subtract,
                                                            ALU.mult))
                        dve.wait_ge(sem(rstd_ready), b + 1)
                        nc.vector.scalar_tensor_tensor(dst, zn[:, b, :], rstd[:, b, 0:1], row(bias), ALU.mult,
                                                       ALU.add).then_inc(sem(signal), 1)

                    def after_attention(a, b):
                        if a > 2:
                            normalized(a, b)
                            return
                        normalized(a, b, which=a)
                        dve.wait_ge(sem(f"res_{a}"), b + 1)
                        statistics(res[:, b, :], b, 1e-5, f"ve_{a}")
                        layernorm(res[:, b, :], xs[:, b, :], f"ln{a + 1}g", f"ln{a + 1}b", b, f"rstd_{a}", f"x{a + 1}")
                        if a == 0:
                            dve.wait_ge(sem("x1"), b + 1)
                            nonzero_rows(xs[:, b, :], 1, b).then_inc(sem("live1"), 1)

                    def attention(a):
                        for s_n, t_n, v_n, o_b in attention_steps(a != 2):
                            if s_n is not None:
                                N = a * G * U + s_n
                                b, u = s_n // U, s_n % U
                                dve.wait_ge(sem("scores_full"), N + 1)
                                ps = scores_ps[:, N % 3, :].rearrange("p (k t) -> p k t", k=HU)
                                if a in (2, 4) and s_n >= 3:
                                    dve.wait_ge(sem("exp_done"), N - 2)
                                if a == 4 and u == 0:
                                    read_out(dve, "mask4", b)
                                if a == 2:
                                    if s_n == 0:
                                        dve.wait_ge(sem("mask1_in"), 16)
                                    for k in range(HU):
                                        ins = nc.vector.tensor_tensor_reduce(
                                            out=masked[:, N % 3, k, :], in0=ps[:, k, :], in1=mask1[:, b, :],
                                            scale=1.0, scalar=-3.4e38, op0=ALU.add, op1=ALU.max,
                                            accum_out=posmax[:, N % 4, k:k + 1])
                                    link(ins)
                                    nc.vector.tensor_scalar(negmax[:, N % 4, :], posmax[:, N % 4, :], -1.0, None,
                                                            ALU.mult).then_inc(sem("max_done"), 1)
                                elif a == 4:
                                    link(nc.vector.tensor_tensor(
                                        masked[:, N % 3, :, :], ps,
                                        fT[:, b, :].unsqueeze(1).to_broadcast([P, HU, S]), ALU.mult))
                                    nc.vector.tensor_scalar(masked[:, N % 3, :, :], masked[:, N % 3, :, :], 50.0,
                                                            -50.0, ALU.min, ALU.max).then_inc(sem("clipped"), 1)
                                else:
                                    nc.vector.tensor_reduce(negmax[:, N % 4, :], ps, AX.X, ALU.max,
                                                            negate=True).then_inc(sem("max_done"), 1)
                            if t_n is not None and a != 4 and (a * G * U + t_n) % 2 == 0:
                                N = a * G * U + t_n
                                dve.wait_ge(sem("probT_full"), N + 1)
                                if N >= 4:
                                    values_done(dve, N - 4)
                                nc.vector.tensor_copy(probT[:, N % 4, :, :].rearrange("p k s -> p (k s)"),
                                                      probT_ps[:, N % 2, :]).then_inc(sem("probT_ready0"), 1)
                            if v_n is not None and a == 2:
                                b, u = v_n // U, v_n % U
                                ps = take(dve, "pv2", v_n)[:, 0:HU * VW1].rearrange("p (k w) -> p k w", k=HU)
                                link(nc.vector.reciprocal(rden[:, b, u * HU:(u + 1) * HU], ps[:, :, HD]))
                                ins = nc.vector.tensor_tensor(
                                    nat[:, b, u * D:(u + 1) * D].rearrange("p (k d) -> p k d", k=HU), ps[:, :, 0:HD],
                                    rden[:, b, u * HU:(u + 1) * HU].unsqueeze(2).to_broadcast([P, HU, HD]), ALU.mult)
                                release(ins, "pv2", v_n)
                            if o_b is not None:
                                after_attention(a, o_b)

                    dve.wait_ge(sem("x_in"), 16)
                    for b in range(G):
                        link(nonzero_rows(xs[:, b, :], 0, b))
                    for b in range(G + 1):
                        if b < G:
                            per_head(0, b)
                            first_query(0, b)
                        if b:
                            length_penalty(0, b - 1)
                    dve.wait_ge(sem("ctx_in"), 16)
                    for b in range(G):
                        link(nc.vector.bn_stats(cst[:, b, :], ctx[:, b, :]))
                        link(nc.vector.bn_aggr(cmv[:, b, :], cst[:, b, :]))
                        link(nc.vector.tensor_scalar(cve[:, b, 0:1], cmv[:, b, 1:2], 1e-5, None, ALU.add))
                        link(nc.vector.scalar_tensor_tensor(cve[:, b, 1:2], cmv[:, b, 0:1], cmv[:, b, 0:1],
                                                            cmv[:, b, 1:2], ALU.mult, ALU.add))
                        nc.vector.tensor_scalar(cve[:, b, 1:2], cve[:, b, 1:2], 1e-6, None, ALU.add)\
                            .then_inc(sem("cve"), 1)
                    attention(0)
                    for b in range(G + 1):
                        if b < G:
                            per_head(1, b)
                            first_query(1, b)
                        if b:
                            length_penalty(1, b - 1)
                    attention(1)
                    for b in range(G):
                        ps = take(dve, "z", b)
                        ins = nc.vector.tensor_tensor(zn[:, b, :], ps[:, 0:D], row("fc2b"), ALU.add)
                        release(ins, "z", b)
                        read_out(dve, "z", b)
                        link(nc.vector.scalar_tensor_tensor(res[:, b, :], zn[:, b, :], live[:, 0, b:b + 1],
                                                            xs[:, b, :], ALU.mult, ALU.add))
                        statistics(res[:, b, :], b, 1e-5, "ve_m")
                        layernorm(res[:, b, :], xs[:, b, :], "ln3g", "ln3b", b, "rstd_m", "x3")

                    def rms(b, sums, signal, rstd_ready, out_signal, phase):
                        if phase == 0:
                            dve.wait_ge(sem(sums), b + 1)
                            nc.vector.tensor_scalar(ve[:, b, 0:1], ssq[:, b:b + 1], 1.0 / D, 1e-6, ALU.mult, ALU.add)\
                                .then_inc(sem(signal), 1)
                        else:
                            dve.wait_ge(sem(rstd_ready), b + 1)
                            nc.vector.tensor_scalar(zn[:, b, :], xs[:, b, :], rstd[:, b, 0:1], None, ALU.mult)\
                                .then_inc(sem(out_signal), 1)

                    for b in range(G + 1):
                        if b < G:
                            rms(b, "ssq3", "ve_2", "rstd_2", "n3", 0)
                        if b:
                            rms(b - 1, "ssq3", "ve_2", "rstd_2", "n3", 1)
                    for b in range(G + 1):
                        if b < G:
                            for k, name in enumerate(["q2a", "q2b", "kv2"]):
                                m = 3 * b + k
                                heads = 8 if k < 2 else NKV
                                cos, sin = (const("cosq"), const("sinq")) if k < 2 else (const("cosk"), const("sink"))
                                full = take(dve, name, b)
                                if k == 2:
                                    nc.vector.tensor_copy(v64[:, b, :, 0:HD],
                                                          full[:, 256:512].rearrange("p (g d) -> p g d", g=NKV))
                                ps = full[:, 0:heads * HD].rearrange("p (h r d) -> p h r d", h=heads, r=2)
                                if m >= 2:
                                    dve.wait_ge(sem("roped"), m - 1)
                                t1 = ropes[:, m % 2, 0:heads * HD]
                                t2 = ropes[:, 2 + m % 2, 0:heads * HD].rearrange("p (h r d) -> p h r d", h=heads, r=2)
                                nc.vector.tensor_tensor(t1.rearrange("p (h d) -> p h d", h=heads),
                                                        ps.rearrange("p h r d -> p h (r d)"),
                                                        cos.unsqueeze(1).to_broadcast([P, heads, HD]), ALU.mult)
                                for r in range(2):
                                    half = sin[:, r * 32:(r + 1) * 32].unsqueeze(1).to_broadcast([P, heads, 32])
                                    ins = nc.vector.tensor_tensor(t2[:, :, r, :], ps[:, :, 1 - r, :], half, ALU.mult)
                                release(ins, name, b)
                        if b:
                            ps = take(dve, "kT2", b - 1)
                            ins = nc.vector.tensor_copy(plainT[:, b - 1, :, :].rearrange("p c s -> p (c s)"), ps[:, 0:D])
                            release(ins, "kT2", b - 1)
                    attention(2)
                    for b in range(G + 1):
                        if b < G:
                            ps = take(dve, "aTb", b)
                            ins = nc.vector.tensor_copy(tr[:, b, 4:8, :].rearrange("p c s -> p (c s)"), ps)
                            release(ins, "aTb", b)
                        if b:
                            ps = take(dve, "o2", b - 1)
                            ins = nc.vector.tensor_tensor(xs[:, b - 1, :], ps[:, 0:D], xs[:, b - 1, :], ALU.add)
                            release(ins, "o2", b - 1)
                    for b in range(G + 1):
                        if b < G:
                            rms(b, "ssqh", "ve_h", "rstd_h", "n_h", 0)
                        if b:
                            rms(b - 1, "ssqh", "ve_h", "rstd_h", "n_h", 1)
                    for b in range(G + 1):
                        if b < G:
                            for k in range(2):
                                dve.wait_ge(sem("tanh"), 2 * b + k + 1)
                                ps = take(dve, f"g{k}", b)
                                ins = nc.vector.scalar_tensor_tensor(
                                    masked[:, k, :, :].rearrange("p k s -> p (k s)"),
                                    prob[:, k, :, :].rearrange("p k s -> p (k s)"), 1.0, ps, ALU.add, ALU.mult)
                                release(ins, f"g{k}", b)
                                read_out(dve, f"g{k}", b)
                                ps = take(dve, f"u{k}", b)
                                ins = nc.vector.scalar_tensor_tensor(
                                    tr[:, b, 4 * k:4 * k + 4, :].rearrange("p c s -> p (c s)"),
                                    masked[:, k, :, :].rearrange("p k s -> p (k s)"), 0.5, ps, ALU.mult, ALU.mult)
                                release(ins, f"u{k}", b)
                        if b:
                            ps = take(dve, "dn", b - 1)
                            ins = nc.vector.tensor_tensor(xs[:, b - 1, :], ps[:, 0:D], xs[:, b - 1, :], ALU.add)
                            release(ins, "dn", b - 1)
                            read_out(dve, "dn", b - 1)
                            statistics(xs[:, b - 1, :], b - 1, 1e-5, "ve_4")
                            dve.wait_ge(sem("rstd_4"), b)
                            nc.vector.tensor_scalar(zn[:, b - 1, :], xs[:, b - 1, :], mv[:, b - 1, 0:1],
                                                    rstd[:, b - 1, 0:1], ALU.subtract, ALU.mult)\
                                .then_inc(sem("n4"), 1)
                    for b in range(G):
                        per_head(3, b)
                    attention(3)
                    for b in range(G):
                        ps = take(dve, "o3", b)
                        dve.wait_ge(sem("res_3"), b + 1)
                        ins = nc.vector.tensor_tensor(xs[:, b, :], ps[:, 0:D], res[:, b, :], ALU.add)
                        release(ins, "o3", b)
                    for b in range(G):
                        ps = take(dve, "mask4", b)
                        ins = nc.vector.tensor_scalar(fT[:, b, :], ps[:, 0:S], 0.5, 0.5, ALU.mult, ALU.add)
                        release(ins, "mask4", b)
                        read_out(dve, "mask4", b)
                    for b in range(G):
                        per_head(4, b)
                    attention(4)
                    for b in range(G):
                        ps = take(dve, "o4", b)
                        dve.wait_ge(sem("res_4"), b + 1)
                        ins = nc.vector.tensor_tensor(xs[:, b, :], ps[:, 0:D], res[:, b, :], ALU.add)
                        release(ins, "o4", b)
                        read_out(dve, "o4", b)
                        statistics(xs[:, b, :], b, 1e-5, "ve_5")
                        layernorm(xs[:, b, :], outn[:, b, :], "gamma", "beta", b, "rstd_5", "out_ready")

            for name in sorted(set(names) - setup_names | {n for n in names if n.startswith("bank_")}):
                nc.sync.sem_clear(names[name])
            with nc.Block() as block:
                @block.sync
                def _(sp):
                    sp.nop()


def pack(w):
    k, n = w.shape
    return w.reshape(k // P, P, n).transpose(1, 0, 2).reshape(P, -1)


def grouped_heads(w):
    return w.reshape(-1, 2, 2, 4, HD).transpose(0, 1, 3, 2, 4).reshape(-1, FF)


def by_head(w):
    return w.transpose(1, 0, 2).reshape(D, D)


def shape_constants():
    f = np.float32
    p = np.arange(P)
    inv_freq = (f(1.0) / f(10000.0) ** (np.arange(0, HD, 2, dtype=f) / f(HD))).astype(f)
    angle = p.astype(f)[:, None] * inv_freq[None, :]
    cos, sin = np.cos(angle), np.sin(angle)
    cos2, sin2 = np.concatenate([cos, cos], 1), np.concatenate([-sin, sin], 1)
    head8 = (p[:, None] // 16 == np.arange(8)[None, :]).astype(f)
    bd = np.zeros((P, C, C, 8), f)
    for c in range(C):
        bd[:, c, c, :] = head8
    parts = {"ident": np.eye(P, dtype=f), "causal": np.where(p[None, :] > p[:, None], f(MASKED), f(0.0)),
             "iota": np.broadcast_to(p.astype(f), (P, P)), "cosq": cos2 / f(8), "sinq": sin2 / f(8), "cosk": cos2,
             "sink": sin2, "head8": head8, "head8q": head8 * f(0.25),
             "bd": bd.reshape(P, -1), "expo": np.full((P, 2), -0.5, f)}
    return np.ascontiguousarray(np.concatenate([parts[n].astype(f) for n, _ in CONSTS], 1))


def kernel(**inputs):
    import concourse.bacc as bacc
    from concourse.bass_utils import run_bass_kernel_spmd

    a = {k: np.asarray(v) for k, v in inputs.items()}
    l0, l1, l2, l3 = "L0_xattn_", "L1_xattn_", "L2_xattn_", "L3_xattn_"
    cat = np.concatenate
    weights = {
        "qk0": cat([by_head(a[l0 + "Wq1"]), by_head(a[l0 + "Wk1"])], 1),
        "v0": by_head(a[l0 + "Wv1"]),
        "qk1": cat([by_head(a[l0 + "Wq2"]), by_head(a[l0 + "Wk2"])], 1),
        "v1": by_head(a[l0 + "Wv2"]), "fc1": a[l0 + "fc1_w"].T, "fc2": a[l0 + "fc2_w"].T,
        "q2": grouped_heads(a[l1 + "Wq"]), "kv2": cat([a[l1 + "Wk"], a[l1 + "Wv"]], 1), "o2": a[l1 + "Wo"],
        "gate": a[l1 + "Wgate"], "up": a[l1 + "Wup"], "down": a[l1 + "Wdown"],
        "qk3": cat([a[l2 + "Wq"], a[l2 + "Wk"]], 1), "v3": a[l2 + "Wv"],
        "o3": a[l2 + "Wo"],
        "qk4": cat([a[l3 + "Wq"], a[l3 + "Wk"]], 1), "v4": a[l3 + "Wv"],
        "o4": a[l3 + "Wo"]}
    rows = {"ln1g": a[l0 + "ln1_g"], "ln1b": a[l0 + "ln1_b"], "ln2g": a[l0 + "ln2_g"], "ln2b": a[l0 + "ln2_b"],
            "ln3g": a[l0 + "ln3_g"], "ln3b": a[l0 + "ln3_b"], "fc2b": a[l0 + "fc2_b"], "bo3": a[l2 + "bo"],
            "bo4": a[l3 + "bo"], "gamma": a[l3 + "gamma"], "beta": a[l3 + "beta"]}
    cols = {"fc1b": a[l0 + "fc1_b"], "rms1": a[l1 + "ln1_w"], "rms2": a[l1 + "ln2_w"],
            "bq3": a[l2 + "bq"], "bk3": a[l2 + "bk"],
            "bv3": a[l2 + "bv"], "gq": a[l2 + "gq"], "betaq": a[l2 + "betaq"], "gkv": a[l2 + "gkv"],
            "betakv": a[l2 + "betakv"], "bq4": a[l3 + "bq"],
            "bk4": a[l3 + "bk"], "bv4": a[l3 + "bv"]}
    arrays = {
        "x": a["x"], "ctx": a["ctx_1024"], "mask1": a["mask_Bx1xSxS2_ff0"], "mask3": a["mask_Bx1xSxS2_fk0"],
        "weights": cat([pack(weights[n]) for n, _ in WEIGHTS], 1),
        "rows": np.broadcast_to(cat([rows[n] for n in ROWS])[None, :], (P, R_ALL)),
        "cols": cat([cols[n].reshape(C, P).T for n in COLS], 1),
        "consts": shape_constants()}
    arrays = {k: np.ascontiguousarray(v) for k, v in arrays.items()}

    nc = bacc.Bacc("TRN2", target_bir_lowering=False, num_devices=1)
    aps = [nc.dram_tensor(f"{k}_dram", v.shape, mybir.dt.from_np(v.dtype), kind="ExternalInput").ap() for k, v in arrays.items()]
    out = nc.dram_tensor("out_dram", (B, S, D), mybir.dt.float32, kind="ExternalOutput").ap()
    build(nc, *aps, out)
    r = run_bass_kernel_spmd(nc, [{f"{k}_dram": v for k, v in arrays.items()}], core_ids=[0])
    return r.results[0]["out_dram"]
```

```python
from contextlib import ExitStack

import numpy as np

import concourse.bass as bass
from concourse import mybir

P = 128
B = 64
S = 128
D = 256
C = D // P
H = 16
G = 4
NG = B // G
U = 4
HU = H // U
FF = 1024
FB = FF // P
NKV = 4
HD = FF // H
VW = 32
VW1 = HD + 2
MASKED = -1.0e30

WEIGHTS = [("qk0", 2 * 512), ("v0", 2 * 256), ("qk1", 2 * 512), ("v1", 2 * 256), ("fc1", 2 * 256), ("fc2", 2 * 256),
           ("q2", 2 * 1024), ("kv2", 2 * 512), ("o2", 8 * 256), ("gate", 2 * 1024), ("up", 2 * 1024),
           ("down", 8 * 256), ("qk3", 2 * 512), ("v3", 2 * 256), ("o3", 2 * 256), ("qk4", 2 * 512), ("v4", 2 * 256),
           ("o4", 2 * 256)]
ROWS = ["ln1g", "ln1b", "ln2g", "ln2b", "ln3g", "ln3b", "fc2b", "bo3", "bo4", "gamma", "beta"]
COLS = ["fc1b", "rms1", "rms2", "bq3", "bk3", "bv3", "gq", "betaq", "gkv", "betakv", "bq4", "bk4", "bv4"]
CONSTS = [("ident", 128), ("causal", 128), ("iota", 128), ("cosq", 64), ("sinq", 64), ("cosk", 64), ("sink", 64),
          ("head8", 8), ("head8q", 8), ("bd", 32), ("expo", 2)]


def offsets(items):
    at, out = 0, {}
    for name, width in items:
        out[name] = (at, width)
        at += width
    return out, at


W_OFF, W_ALL = offsets(WEIGHTS)
R_OFF, R_ALL = offsets([(n, D) for n in ROWS])
K_OFF, K_ALL = offsets([(n, C) for n in COLS])
C_OFF, C_ALL = offsets(CONSTS)


T_LAG = 3
PV_LAG = [4, 4, 4, 4, 3]
FIRST_STEP = [0, 17, 40, 61, 77]
BETWEEN = [
    [(9, "attended", 0), (10, "stats", 0), (11, "norm", 0), (12, "ctx_norms", 0), (13, "tr", 1), (14, "proj", 1),
     (15, "first_row", 1)],
    [(9, "attended", 1), (10, "stats", 1), (11, "norm", 1), (13, "x2T", 1), (14, "h", 1), (15, "z", 1),
     (16, "norm_x3", 1), (17, "mean_square", 2), (18, "rms_norm", 2), (19, "tr", 2), (20, "q2", 2), (21, "kv2", 2),
     (22, "rotatedT", 2)],
    [(8, "aT", 0), (9, "aT", 1), (10, "o2", 2), (11, "mean_square", 3), (12, "rms_norm", 3), (13, "nT", 3),
     (14, "gate_up", 0), (15, "gate_up", 1), (16, "down", 3), (17, "norm_x4", 3), (18, "tr", 3), (19, "proj", 3)],
    [(3, "mask4", 4), (9, "attended", 3), (10, "zT", 3), (11, "o", 3), (13, "tr", 4), (14, "proj", 4)],
    [(4, "xT", 0), (7, "proj", 0), (8, "attended", 4), (9, "zT", 4), (9, "first_row", 0), (10, "o", 4),
     (11, "norm", 4)],
]


def schedule():
    steps = {}

    def put(step, name, a, i):
        steps.setdefault(step, []).append((name, a, i))

    for name in ["turn", "values", "scores"]:
        for a in range(5):
            lag = {"scores": 0, "turn": T_LAG, "values": PV_LAG[a]}[name]
            for n in range(G * U):
                if not (a == 4 and name == "turn"):
                    put(FIRST_STEP[a] + n + lag, name, a, n)
    for a in range(5):
        for b in range(G):
            for lag, name, k in BETWEEN[a]:
                put(FIRST_STEP[a] + U * b + lag, name, k, b)
    return [event for step in sorted(steps) for event in steps[step]]


SCHEDULE = schedule()
PROLOGUE = [(name, 0, b) for b in range(G) for name in ["xT", "proj", "first_row"]]


def bank_uses(name, a):
    if name in ("xT", "x2T", "h", "z", "kv2", "o2", "nT", "mask4"):
        return [name]
    return {"proj": [f"m{a}", f"sv{a}"], "first_row": [f"e{a}"], "attended": [f"on{a}"], "tr": [f"tr{a}"],
            "q2": ["q2a", "q2b"], "rotatedT": ["qT2a", "qT2b", "kT2"], "aT": [f"aT{a}"], "gate_up": [f"g{a}", f"u{a}"],
            "down": ["dn"], "zT": [f"zT{a}"], "o": [f"o{a}"]}.get(name, [])


N_GEN = 3


def count_plan(events):
    uses = [(use, i) for name, a, i in events for use in bank_uses(name, a)]
    return {use: (k % N_GEN, k // N_GEN + 1) for k, use in enumerate(uses)}


def attended_before(N):
    return sum(n // (G * U) == 2 or n % U == U - 1 for n in range(N))


def build(nc, x_d, ctx_d, mask1_d, mask3_d, w_d, rows_d, cols_d, consts_d, out_d):
    fp32, bf16 = mybir.dt.float32, mybir.dt.bfloat16
    ALU, ACT, AX = mybir.AluOpType, mybir.ActivationFunctionType, mybir.AxisListType
    es = ExitStack()
    with es:
        def sb(name, shape, dt=fp32):
            return es.enter_context(nc.sbuf_tensor(name, shape, dt))

        w_sb = sb("w_sb", [P, W_ALL])
        rows_sb = sb("rows_sb", [P, R_ALL])
        cols_sb = sb("cols_sb", [P, K_ALL])
        consts = sb("consts", [P, C_ALL])
        identb = sb("identb", [P, P], bf16)
        causalb = sb("causalb", [P, P], bf16)
        qbias = sb("qbias", [P, 2, C])
        kbias = sb("kbias", [P, 2, C])
        vbias = sb("vbias", [P, 2, C])
        xs = sb("xs", [P, G, D])
        ctx = sb("ctx", [P, G, D])
        ctx_ln = sb("ctx_ln", [P, G, D])
        ctx_rms = sb("ctx_rms", [P, G, D])
        res = sb("res", [P, G, D])
        zn = sb("zn", [P, G, D])
        actT = sb("actT", [P, G, 4, P])
        plainT = sb("plainT", [P, G, C, P])
        v16 = sb("v16", [P, G, H, VW])
        v64 = sb("v64", [P, G, NKV, VW1])
        wide = sb("wide", [P, G, 2 * FF])
        oT = sb("oT", [P, 2, U, S])
        mask1 = sb("mask1", [P, G, S])
        mask3 = sb("mask3", [P, G, S])
        fT = sb("fT", [P, G, S])
        nat = wide[:, :, 0:FF]
        tr = wide[:, :, FF:2 * FF].rearrange("p g (c s) -> p g c s", s=P)
        by_head_T = wide[:, :, :].rearrange("p g (h s) -> p g h s", h=H)
        ctx_m = res
        outn = res
        x_in = ctx_rms
        keys = [ctx_ln, zn]
        prob = sb("prob", [P, 4, HU, S])
        probT = sb("probT", [P, 4, HU, S])
        masked = sb("masked", [P, 3, HU, S])
        negmax = sb("negmax", [P, 4, HU])
        posmax = sb("posmax", [P, 4, HU])
        absmax = sb("absmax", [P, G])
        live = sb("live", [P, 2, G])
        st = sb("st", [P, G, 6])
        mv = sb("mv", [P, G, 2])
        ve = sb("ve", [P, G, 2])
        rstd = sb("rstd", [P, G, 2])
        cst = sb("cst", [P, G, 6])
        cmv = sb("cmv", [P, G, 2])
        cve = sb("cve", [P, G, 2])
        crstd = sb("crstd", [P, G, 2])
        ssq = sb("ssq", [P, G])
        rden = sb("rden", [P, G, H])
        rdenm = sb("rdenm", [P, G, H])
        q0 = sb("q0", [P, G, C, H])
        nz = sb("nz", [H, G, S])
        count = sb("count", [H, G])
        fill = sb("fill", [H, G, 2])
        pen = sb("pen", [P, G, S], bf16)
        scores_ps = es.enter_context(nc.psum_tensor("scores_ps", [P, 3, 512], fp32))
        probT_ps = es.enter_context(nc.psum_tensor("probT_ps", [P, 512], fp32))
        pv_ps = es.enter_context(nc.psum_tensor("pv_ps", [P, 512], fp32))
        gen_ps = es.enter_context(nc.psum_tensor("gen_ps", [P, N_GEN, 512], fp32))

        names = {}

        def sem(name):
            if name not in names:
                names[name] = es.enter_context(nc.semaphore(name))
            return names[name]

        bank_full = [sem(f"bank_full{j}") for j in range(N_GEN)]
        bank_read = [sem(f"bank_read{j}") for j in range(N_GEN)]
        plan = {}

        def W(name):
            at, width = W_OFF[name]
            k = {"o2": 8, "down": 8}.get(name, 2)
            return w_sb[:, at:at + width].rearrange("p (c n) -> p c n", c=k)

        def row(name):
            at, width = R_OFF[name]
            return rows_sb[:, at:at + width]

        def col(name, c):
            at, _ = K_OFF[name]
            return cols_sb[:, at + c:at + c + 1]

        def const(name):
            at, width = C_OFF[name]
            return consts[:, at:at + width]

        ident = const("ident")

        def take(eng, name, i):
            j, use = plan[name, i]
            eng.wait_ge(bank_full[j], use)
            return gen_ps[:, j, :]

        def release(ins, name, i):
            ins.then_inc(bank_read[plan[name, i][0]], 1)

        def read_out(eng, name, i):
            j, use = plan[name, i]
            eng.wait_ge(bank_read[j], use)

        def scores_read(eng, N):
            if N // (G * U) == 2:
                eng.wait_ge(sem("max_done"), N + 1)
            elif N // (G * U) == 4:
                eng.wait_ge(sem("clipped"), N % (G * U) + 1)
            else:
                eng.wait_ge(sem("exp_done"), N + 1)

        def turned(eng, N):
            eng.wait_ge(sem("probT_copied"), N + 1)

        with nc.Block() as block:
            @block.sync
            def _(sp):
                sp.dma_start(consts[:, :], consts_d).then_inc(sem("su_cols"), 16)
                sp.dma_start(cols_sb[:, :], cols_d).then_inc(sem("su_cols"), 16)
                sp.dma_start(rows_sb[:, :], rows_d).then_inc(sem("su_rows"), 16)
                half = W_OFF["q2"][0]
                sp.dma_start(w_sb[:, half:W_ALL], w_d[:, half:W_ALL]).then_inc(sem("su_w"), 16)
                sp.dma_start(w_sb[:, 0:half], w_d[:, 0:half]).then_inc(sem("su_w0"), 16)
                sp.wait_ge(sem("su_w0"), 16)

            @block.gpsimd
            def _(pool):
                pool.memset(v16[:, :, :, :], 0.0).then_inc(sem("su_v"), 1)
                pool.memset(v64[:, :, :, :], 0.0).then_inc(sem("su_v"), 1)
                pool.wait_ge(sem("su_v"), 2)
                pool.memset(v16[:, :, :, 16:17], 1.0).then_inc(sem("su_v"), 1)
                pool.memset(v64[:, :, :, HD:HD + 1], 1.0).then_inc(sem("su_v"), 1)
                pool.memset(pen[:, :, :], 0.0).then_inc(sem("su_v"), 1)
                pool.wait_ge(sem("su_v"), 5)

            @block.tensor
            def _(pe):
                pe.wait_ge(sem("su_w"), 16)
                pe.wait_ge(sem("su_cols"), 32)
                for k, (w, first, beta) in enumerate([("qk3", 0, "betaq"), ("qk3", 256, "betakv"), ("v3", 0, "betakv")]):
                    for n in range(C):
                        for c in range(C):
                            last = nc.tensor.matmul(gen_ps[:, 0, 2 * k + n:2 * k + n + 1],
                                                    W(w)[:, c, first + n * P:first + (n + 1) * P], col(beta, c),
                                                    start=(c == 0), stop=(c == C - 1))
                last.then_inc(sem("su_beta"), 1)
                pe.wait_ge(sem("su_vb"), 1)
                for a in range(2):
                    for c in range(C):
                        last = nc.tensor.matmul(gen_ps[:, 1, a * D:(a + 1) * D], masked[:, c, 0, :]
                                                if a == 0 else probT[:, c, 0, :], W(f"o{3 + a}")[:, c, :],
                                                start=(c == 0), stop=(c == C - 1))
                last.then_inc(sem("su_bo"), 1)

            @block.vector
            def _(dve):
                dve.wait_ge(sem("su_cols"), 32)
                nc.vector.tensor_copy(identb[:, :], ident)
                nc.vector.tensor_copy(causalb[:, :], const("causal"))
                dve.wait_ge(sem("su_beta"), 1)
                own = [0]

                def step(ins):
                    own[0] += 1
                    ins.then_inc(sem("su_dve"), 1)

                for c in range(C):
                    step(nc.vector.tensor_tensor(vbias[:, 0, c:c + 1], gen_ps[:, 0, 4 + c:5 + c], col("bv3", c), ALU.add))
                    step(nc.vector.tensor_copy(vbias[:, 1, c:c + 1], col("bv4", c)))
                    step(nc.vector.tensor_tensor(kbias[:, 0, c:c + 1], gen_ps[:, 0, 2 + c:3 + c], col("bk3", c), ALU.add))
                    step(nc.vector.tensor_copy(kbias[:, 1, c:c + 1], col("bk4", c)))
                    step(nc.vector.tensor_tensor(qbias[:, 0, c:c + 1], gen_ps[:, 0, c:c + 1], col("bq3", c), ALU.add))
                    step(nc.vector.tensor_copy(qbias[:, 1, c:c + 1], col("bq4", c)))
                dve.wait_ge(sem("su_dve"), own[0])
                step(nc.vector.tensor_scalar(qbias[:, 0, :], qbias[:, 0, :], 0.25, None, ALU.mult))
                for a in range(2):
                    for c in range(C):
                        dst = masked[:, c, 0, :] if a == 0 else probT[:, c, 0, :]
                        step(nc.vector.tensor_copy(dst, vbias[:, a, c:c + 1].to_broadcast([P, P])))
                dve.wait_ge(sem("su_dve"), own[0])
                nc.vector.nop().then_inc(sem("su_vb"), 1)
                for w, g in [("q2", "rms1"), ("kv2", "rms1"), ("gate", "rms2"), ("up", "rms2")]:
                    for c in range(C):
                        nc.vector.tensor_scalar(W(w)[:, c, :], W(w)[:, c, :], col(g, c), None, ALU.mult)
                for w, first, g in [("qk3", 0, "gq"), ("qk3", 256, "gkv"), ("v3", 0, "gkv")]:
                    for c in range(C):
                        nc.vector.tensor_scalar(W(w)[:, c, first:first + D], W(w)[:, c, first:first + D], col(g, c),
                                                None, ALU.mult)
                dve.wait_ge(sem("su_rows"), 16)
                dve.wait_ge(sem("su_bo"), 1)
                for a in range(2):
                    ins = nc.vector.tensor_tensor(row(f"bo{3 + a}"), gen_ps[:, 1, a * D:(a + 1) * D],
                                                  row(f"bo{3 + a}"), ALU.add)
                ins.then_inc(sem("su_end"), 1)
                dve.wait_ge(sem("su_end"), 1)

        def tensor_program(pe, events):
            def begin(name, i_):
                j, use = plan[name, i_]
                if use > 1:
                    pe.wait_ge(bank_read[j], use - 1)
                return gen_ps[:, j, :]

            def end(ins, name, i_):
                ins.then_inc(bank_full[plan[name, i_][0]], 1)

            def transposes(name, b, sources):
                ps = begin(name, b)
                for k, src in enumerate(sources):
                    last = nc.tensor.transpose(ps[:, k * P:(k + 1) * P], src, ident)
                end(last, name, b)

            def halves(t):
                return [t[:, c * P:(c + 1) * P] for c in range(C)]

            def product(ps, lhsT, rhs, chunks):
                for c in range(chunks):
                    last = nc.tensor.matmul(ps, lhsT(c), rhs(c), start=(c == 0), stop=(c == chunks - 1))
                return last

            def qkv(a, b):
                kv = 2
                key_first, query_first = (D, kv), (0, 2 if a == 0 else 0)
                moving, plain = (query_first, key_first) if a == 4 else (key_first, query_first)
                for name, (first, src) in [(f"m{a}", moving), (f"sv{a}", plain)]:
                    ps = begin(name, b)
                    for n in range(C):
                        last = product(ps[:, n * P:(n + 1) * P],
                                       lambda c: W(f"qk{a}")[:, c, first + n * P:first + (n + 1) * P],
                                       lambda c: actT[:, b, src + c, :], C)
                    if name[0] == "s":
                        last = product(ps[:, D:2 * D], lambda c: actT[:, b, kv + c, :],
                                       lambda c: W(f"v{a}")[:, c, :], C)
                    end(last, name, b)

            def first_row(a, b):
                pe.wait_ge(sem(f"q0_{a}"), b + 1)
                ps = begin(f"e{a}", b)
                end(product(ps[0:H, 0:S], lambda c: q0[:, b, c, :], lambda c: keys[a][:, b, c * P:(c + 1) * P], C),
                    f"e{a}", b)

            def scores(a, n):
                N = a * G * U + n
                b, u = n // U, n % U
                ps = scores_ps[:, N % 3, :]
                if u == 0 and a > 0:
                    for name in ["qT2a", "qT2b", "kT2"] if a == 2 else [f"m{a}", f"sv{a}"]:
                        read_out(pe, name, b)
                    if a == 1:
                        pe.wait_ge(sem("pen_1"), b + 1)
                if N >= 3:
                    scores_read(pe, N - 3)
                if a == 2:
                    r = (u % 2) * HD
                    for k in range(HU):
                        last = nc.tensor.matmul(ps[:, k * S:(k + 1) * S],
                                                tr[r:r + HD, b, (u // 2) * HU + k, :],
                                                plainT[r:r + HD, b, u // 2, :], start=True, stop=True)
                else:
                    if a == 0:
                        nc.tensor.matmul(ps, identb[:, :],
                                         causalb[:, :].unsqueeze(1).to_broadcast([P, HU, S]),
                                         start=True, stop=False, skip_group_check=True)
                    for k in range(HU if a < 2 else 0):
                        h = HU * u + k
                        nc.tensor.matmul(ps[:, k * S:(k + 1) * S], identb[:, h:h + 1].to_broadcast([P, P]),
                                         pen[:, b, :], start=(a == 1 and k == 0), stop=False,
                                         skip_group_check=True)
                    last = nc.tensor.matmul(ps, plainT[:, b, u // 2, :],
                                            by_head_T[:, b, HU * u:HU * (u + 1), :]
                                            .rearrange("p h s -> p (h s)"), start=(a > 2), stop=True,
                                            skip_group_check=(a < 2))
                last.then_inc(sem("scores_full"), 1)

            def turn(a, n):
                N = a * G * U + n
                pe.wait_ge(sem("exp_done"), N + 1)
                if N:
                    turned(pe, N - 1)
                for k in range(HU):
                    last = nc.tensor.transpose(probT_ps[:, k * S:(k + 1) * S], prob[:, N % 4, k, :], ident)
                last.then_inc(sem("probT_full"), 1)

            def values(a, n):
                N = a * G * U + n
                b, u = n // U, n % U
                if a == 4:
                    pe.wait_ge(sem("exp_done"), N + 1)
                else:
                    turned(pe, N)
                if (a == 2 or u == 0) and N:
                    pe.wait_ge(sem("pv_read"), attended_before(N))
                for k in range(HU):
                    if a == 2:
                        last = nc.tensor.matmul(pv_ps[:, k * VW1:(k + 1) * VW1], probT[:, N % 4, k, :],
                                                v64[:, b, u, :], start=True, stop=True)
                    else:
                        last = nc.tensor.matmul(pv_ps[32 * k:32 * k + 32, u * S:(u + 1) * S],
                                                v16[:, b, HU * u + k, :], probT[:, N % 4, k, :],
                                                start=True, stop=True)
                last.then_inc(sem("values_done"), 1)

            for name, a, i_ in events:
                b = i_
                if name == "scores":
                    scores(a, i_)
                elif name == "turn":
                    turn(a, i_)
                elif name == "values":
                    values(a, i_)
                elif name == "xT":
                    if b == 0:
                        pe.wait_ge(sem("x_in"), 16)
                    transposes("xT", b, halves(x_in[:, b, :]))
                elif name == "proj":
                    read_out(pe, f"tr{a}" if a else "xT", b)
                    qkv(a, b)
                elif name == "first_row":
                    first_row(a, b)
                elif name == "attended":
                    pe.wait_ge(sem("pv_read"), attended_before(a * G * U + U * (b + 1)))
                    transposes(f"on{a}", b, [oT[:, b % 2, u, :] for u in range(U)])
                elif name == "tr" and a == 1:
                    pe.wait_ge(sem("x1"), b + 1)
                    pe.wait_ge(sem("ctx_m"), b + 1)
                    transposes("tr1", b, halves(xs[:, b, :]) + halves(ctx_m[:, b, :]))
                elif name == "tr" and a == 2:
                    pe.wait_ge(sem("n3"), b + 1)
                    pe.wait_ge(sem("ctx_rms"), b + 1)
                    transposes("tr2", b, halves(zn[:, b, :]) + halves(ctx_rms[:, b, :]))
                elif name == "tr" and a == 3:
                    pe.wait_ge(sem("n4"), b + 1)
                    pe.wait_ge(sem("ctx_ln"), b + 1)
                    transposes("tr3", b, halves(zn[:, b, :]) + halves(ctx_ln[:, b, :]))
                elif name == "tr" and a == 4:
                    read_out(pe, "o3", b)
                    transposes("tr4", b, halves(xs[:, b, :]) + halves(ctx[:, b, :]))
                elif name == "mask4":
                    if b == 0:
                        pe.wait_ge(sem("mask3_in"), 16)
                    transposes("mask4", b, [mask3[:, b, :]])
                elif name == "x2T":
                    pe.wait_ge(sem("x2"), b + 1)
                    transposes("x2T", b, halves(xs[:, b, :]))
                elif name == "h":
                    read_out(pe, "x2T", b)
                    ps = begin("h", b)
                    for n in range(C):
                        last = product(ps[:, n * P:(n + 1) * P], lambda c: W("fc1")[:, c, n * P:(n + 1) * P],
                                       lambda c: actT[:, b, c, :], C)
                    end(last, "h", b)
                elif name == "z":
                    read_out(pe, "h", b)
                    ps = begin("z", b)
                    end(product(ps[:, 0:D], lambda c: actT[:, b, 2 + c, :], lambda c: W("fc2")[:, c, :], C),
                        "z", b)
                elif name == "q2":
                    read_out(pe, "tr2", b)
                    for k, use in enumerate(["q2a", "q2b"]):
                        ps = begin(use, b)
                        end(product(ps, lambda c: actT[:, b, c, :],
                                    lambda c: W("q2")[:, c, k * 512:(k + 1) * 512], C), use, b)
                elif name == "kv2":
                    ps = begin("kv2", b)
                    end(product(ps, lambda c: actT[:, b, 2 + c, :], lambda c: W("kv2")[:, c, :], C), "kv2", b)
                elif name == "rotatedT":
                    for k, use in enumerate(["qT2a", "qT2b"]):
                        pe.wait_ge(sem("roped"), 3 * b + k + 1)
                        transposes(use, b, [nat[:, b, (4 * k + m) * P:(4 * k + m + 1) * P] for m in range(4)])
                    pe.wait_ge(sem("roped"), 3 * b + 3)
                    transposes("kT2", b, halves(res[:, b, :]))
                elif name == "aT":
                    pe.wait_ge(sem("pv_read"), attended_before(2 * G * U + U * b + 2 * a + 1) + 1)
                    transposes(f"aT{a}", b, [nat[:, b, (4 * a + m) * P:(4 * a + m + 1) * P] for m in range(4)])
                elif name == "o2":
                    read_out(pe, "aT0", b)
                    read_out(pe, "aT1", b)
                    ps = begin("o2", b)
                    end(product(ps[:, 0:D], lambda c: tr[:, b, c, :], lambda c: W("o2")[:, c, :], FB), "o2", b)
                elif name == "nT":
                    pe.wait_ge(sem("n_h"), b + 1)
                    transposes("nT", b, halves(zn[:, b, :]))
                elif name == "gate_up":
                    read_out(pe, "nT", b)
                    for use, w in [(f"g{a}", "gate"), (f"u{a}", "up")]:
                        ps = begin(use, b)
                        for m in range(4):
                            f = (4 * a + m) * P
                            last = product(ps[:, m * P:(m + 1) * P], lambda c: W(w)[:, c, f:f + P],
                                           lambda c: actT[:, b, c, :], C)
                        end(last, use, b)
                elif name == "down":
                    read_out(pe, "u0", b)
                    read_out(pe, "u1", b)
                    ps = begin("dn", b)
                    end(product(ps[:, 0:D], lambda c: tr[:, b, c, :], lambda c: W("down")[:, c, :], FB),
                        "dn", b)
                elif name == "zT":
                    read_out(pe, f"on{a}", b)
                    transposes(f"zT{a}", b, halves(zn[:, b, :]))
                elif name == "o":
                    read_out(pe, f"zT{a}", b)
                    ps = begin(f"o{a}", b)
                    end(product(ps[:, 0:D], lambda c: actT[:, b, c, :], lambda c: W(f"o{a}")[:, c, :], C),
                        f"o{a}", b)

        def scalar_program(act, events):
            def copy_out(name, b, dst, width):
                release(nc.scalar.activation(dst, take(act, name, b)[:, 0:width], ACT.Copy), name, b)

            def plain_out(a, b):
                ps = take(act, f"sv{a}", b)
                if a < 2:
                    nc.scalar.activation(plainT[:, b, :, :].rearrange("p c s -> p (c s)"), ps[:, 0:D],
                                         ACT.Copy, scale=0.25)
                else:
                    for c in range(C):
                        bias, scale = (qbias[:, 0, c:c + 1], 0.25) if a == 3 else (kbias[:, 1, c:c + 1], 1.0)
                        nc.scalar.activation(plainT[:, b, c, :], ps[:, c * P:(c + 1) * P], ACT.Identity,
                                             bias=bias, scale=scale)
                release(nc.scalar.activation(v16[:, b, :, 0:16],
                                             ps[:, D:2 * D].rearrange("p (h d) -> p h d", h=H), ACT.Copy),
                        f"sv{a}", b)

            def exponentials(a, n):
                N = a * G * U + n
                if a == 4:
                    act.wait_ge(sem("clipped"), n + 1)
                    act.wait_ge(sem("values_done"), N - 3)
                    nc.scalar.activation(probT[:, N % 4, :, :], masked[:, N % 3, :, :],
                                         ACT.Exp).then_inc(sem("exp_done"), 1)
                    return
                act.wait_ge(sem("max_done"), N + 1)
                if N >= 4:
                    act.wait_ge(sem("probT_full"), N - 3)
                src = masked[:, N % 3, :, :] if a == 2 else \
                    scores_ps[:, N % 3, :].rearrange("p (k t) -> p k t", k=HU)
                for k in range(HU):
                    ins = nc.scalar.activation(prob[:, N % 4, k, :], src[:, k, :], ACT.Exp,
                                               bias=negmax[:, N % 4, k:k + 1])
                ins.then_inc(sem("exp_done"), 1)

            def flat(t):
                return t.rearrange("p c s -> p (c s)")

            for name, a, i_ in events:
                b = i_
                if name == "scores":
                    exponentials(a, i_)
                elif name == "turn":
                    N = a * G * U + i_
                    act.wait_ge(sem("probT_full"), N + 1)
                    if N >= 4:
                        act.wait_ge(sem("values_done"), N - 3)
                    nc.scalar.activation(flat(probT[:, N % 4, :, :]), probT_ps[:, :], ACT.Copy)\
                        .then_inc(sem("probT_copied"), 1)
                elif name == "values" and a != 2 and i_ % U == U - 1:
                    act.wait_ge(sem("values_done"), a * G * U + i_ + 1)
                    nc.scalar.activation(flat(oT[:, (i_ // U) % 2, :, :]), pv_ps[:, :], ACT.Copy)\
                        .then_inc(sem("pv_read"), 1)
                elif name == "xT":
                    copy_out("xT", b, flat(actT[:, b, 2:4, :]), D)
                elif name in ("x2T", "nT", "zT"):
                    copy_out(bank_uses(name, a)[0], b, flat(actT[:, b, 0:2, :]), D)
                elif name == "tr":
                    copy_out(f"tr{a}", b, flat(actT[:, b, :, :]), 512)
                elif name == "proj":
                    plain_out(a, b)
                elif name == "h":
                    ps = take(act, "h", b)
                    for c in range(C):
                        ins = nc.scalar.activation(actT[:, b, 2 + c, :], ps[:, c * P:(c + 1) * P], ACT.Relu,
                                                   bias=col("fc1b", c))
                    release(ins, "h", b)
                elif name in ("norm_x3", "o2"):
                    if name == "norm_x3":
                        act.wait_ge(sem("x3"), b + 1)
                    else:
                        read_out(act, "o2", b)
                    nc.scalar.activation(res[:, b, :], xs[:, b, :], ACT.Square, accum_out=ssq[:, b:b + 1])\
                        .then_inc(sem("ssq3" if name == "norm_x3" else "ssqh"), 1)
                elif name == "rotatedT":
                    copy_out("qT2a", b, flat(tr[:, b, 0:4, :]), 512)
                    copy_out("qT2b", b, flat(tr[:, b, 4:8, :]), 512)
                elif name == "aT" and a == 0:
                    copy_out("aT0", b, flat(tr[:, b, 0:4, :]), 512)
                elif name == "gate_up":
                    ps = take(act, f"g{a}", b)
                    nc.scalar.activation(nat[:, b, a * 512:(a + 1) * 512], ps, ACT.Tanh, scale=0.5)\
                        .then_inc(sem("tanh"), 1)

        def gpsimd_program(pool, events):
            def rsqrt(src, dst, wait, signal, b, width=1):
                pool.wait_ge(sem(wait), b + 1)
                nc.gpsimd.tensor_tensor(dst, src, const("expo")[:, 0:width], ALU.pow)\
                    .then_inc(sem(signal), 1)

            def add_residual(a, b):
                read_out(pool, f"on{a}", b)
                nc.gpsimd.tensor_tensor(res[:, b, :], zn[:, b, :], (xs if a else x_in)[:, b, :], ALU.add)\
                    .then_inc(sem(f"res_{a}"), 1)

            for name, a, b in events:
                if name == "ctx_norms":
                    rsqrt(cve[:, b, :], crstd[:, b, :], "cve", "crstd", b, 2)
                    pool.wait_ge(sem("crstd"), b + 1)
                    nc.gpsimd.tensor_scalar(ctx_ln[:, b, :], ctx[:, b, :], cmv[:, b, 0:1], crstd[:, b, 0:1],
                                            ALU.subtract, ALU.mult).then_inc(sem("ctx_ln"), 1)
                    nc.gpsimd.tensor_scalar(ctx_rms[:, b, :], ctx[:, b, :], crstd[:, b, 1:2], 0.0,
                                            ALU.mult, ALU.add).then_inc(sem("ctx_rms"), 1)
                elif name == "attended" and a < 2:
                    add_residual(a, b)
                elif name == "stats":
                    rsqrt(ve[:, b, 0:1], rstd[:, b, 0:1], f"ve_{a}", f"rstd_{a}", b)
                elif name == "norm" and a == 0:
                    if b == 0:
                        pool.wait_ge(sem("ctx_in"), 16)
                    pool.wait_ge(sem("live1"), b + 1)
                    nc.gpsimd.tensor_scalar(ctx_m[:, b, :], ctx[:, b, :], live[:, 1, b:b + 1], 0.0,
                                            ALU.mult, ALU.add).then_inc(sem("ctx_m"), 1)
                elif name == "z":
                    rsqrt(ve[:, b, 0:1], rstd[:, b, 0:1], "ve_m", "rstd_m", b)
                elif name == "mean_square":
                    tag = "2" if a == 2 else "h"
                    rsqrt(ve[:, b, 0:1], rstd[:, b, 0:1], f"ve_{tag}", f"rstd_{tag}", b)
                elif name in ("q2", "kv2"):
                    for k, use in enumerate(bank_uses(name, a)):
                        read_out(pool, use, b)
                        if name == "q2":
                            dst, other = nat[:, b, k * 512:(k + 1) * 512], wide[:, b, FF + k * 512:FF + (k + 1) * 512]
                        else:
                            dst, other = res[:, b, :], zn[:, b, :]
                        nc.gpsimd.tensor_tensor(dst, dst, other, ALU.add).then_inc(sem("roped"), 1)
                elif name == "down":
                    rsqrt(ve[:, b, 0:1], rstd[:, b, 0:1], "ve_4", "rstd_4", b)
                    nc.gpsimd.tensor_tensor(res[:, b, :], xs[:, b, :], row("bo3"), ALU.add)\
                        .then_inc(sem("res_3"), 1)
                elif name == "o" and a == 3:
                    read_out(pool, "o3", b)
                    nc.gpsimd.tensor_tensor(res[:, b, :], xs[:, b, :], row("bo4"), ALU.add)\
                        .then_inc(sem("res_4"), 1)
                elif name == "o" and a == 4:
                    rsqrt(ve[:, b, 0:1], rstd[:, b, 0:1], "ve_5", "rstd_5", b)

        def vector_program(dve, events):
            own = [0]

            def link(ins):
                own[0] += 1
                ins.then_inc(sem("dve_own"), 1)
                dve.wait_ge(sem("dve_own"), own[0])

            def nonzero_rows(src, which, b):
                link(nc.vector.tensor_reduce(absmax[:, b:b + 1], src, AX.X, ALU.max,
                                             apply_absolute_value=True))
                return nc.vector.tensor_scalar(live[:, which, b:b + 1], absmax[:, b:b + 1], 0.0, None,
                                               ALU.is_gt)

            def per_head(a, b):
                ps = take(dve, f"m{a}", b)
                own_rows = const("head8q" if a == 4 else "head8").unsqueeze(2).to_broadcast([P, 8, S])
                for c in range(C):
                    src = ps[:, c * P:(c + 1) * P].unsqueeze(1).to_broadcast([P, 8, S])
                    dst = by_head_T[:, b, 8 * c:8 * c + 8, :]
                    if a < 2:
                        nc.vector.tensor_tensor(dst, src, own_rows, ALU.mult)
                    else:
                        bias = kbias[:, 0, c:c + 1] if a == 3 else qbias[:, 1, c:c + 1]
                        ins = nc.vector.scalar_tensor_tensor(dst, src, bias, own_rows, ALU.add, ALU.mult)
                if a < 2:
                    ins = nc.vector.tensor_copy(keys[a][:, b, :], ps[:, 0:D])
                release(ins, f"m{a}", b)

            def first_query(a, b):
                read_out(dve, f"sv{a}", b)
                nc.vector.tensor_tensor(q0[:, b, :, :], const("bd").rearrange("p (c h) -> p c h", c=C),
                                        plainT[:, b, :, 0:1].to_broadcast([P, C, H]), ALU.mult)\
                    .then_inc(sem(f"q0_{a}"), 1)

            def length_penalty(a, b):
                ps = take(dve, f"e{a}", b)
                ins = nc.vector.tensor_scalar(nz[:, b, :], ps[0:H, 0:S], 0.0, None, ALU.not_equal)
                release(ins, f"e{a}", b)
                read_out(dve, f"e{a}", b)
                link(nc.vector.tensor_reduce(count[:, b:b + 1], nz[:, b, :], AX.X, ALU.add))
                link(nc.vector.tensor_scalar(fill[:, b, 0:1], count[:, b:b + 1], 0.5, -3.0e38, ALU.is_lt,
                                             ALU.mult))
                link(nc.vector.tensor_scalar(fill[:, b, 1:2], fill[:, b, 0:1], 1.0e10, MASKED, ALU.mult,
                                             ALU.add))
                nc.vector.tensor_scalar(pen[0:H, b, :], const("iota")[0:H, :], count[:, b:b + 1],
                                        fill[:, b, 1:2], ALU.is_ge, ALU.mult).then_inc(sem(f"pen_{a}"), 1)

            def normalized(a, b, which=None):
                ps = take(dve, f"on{a}", b).rearrange("p (h w) -> p h w", h=H)
                link(nc.vector.reciprocal(rden[:, b, :], ps[:, :, 16]))
                rec = rden
                if which is not None:
                    link(nc.vector.tensor_scalar(rdenm[:, b, :], rden[:, b, :], live[:, which, b:b + 1], None,
                                                 ALU.mult))
                    rec = rdenm
                ins = nc.vector.tensor_tensor(zn[:, b, :].rearrange("p (h d) -> p h d", h=H), ps[:, :, 0:16],
                                              rec[:, b, :].unsqueeze(2).to_broadcast([P, H, 16]), ALU.mult)
                release(ins, f"on{a}", b)

            def statistics(src, b, eps, signal):
                link(nc.vector.bn_stats(st[:, b, :], src))
                link(nc.vector.bn_aggr(mv[:, b, :], st[:, b, :]))
                nc.vector.tensor_scalar(ve[:, b, 0:1], mv[:, b, 1:2], eps, None, ALU.add)\
                    .then_inc(sem(signal), 1)

            def layernorm(src, dst, gain, bias, b, rstd_ready, signal):
                link(nc.vector.scalar_tensor_tensor(zn[:, b, :], src, mv[:, b, 0:1], row(gain), ALU.subtract,
                                                    ALU.mult))
                dve.wait_ge(sem(rstd_ready), b + 1)
                nc.vector.scalar_tensor_tensor(dst, zn[:, b, :], rstd[:, b, 0:1], row(bias), ALU.mult,
                                               ALU.add).then_inc(sem(signal), 1)

            def scores_out(a, n):
                N = a * G * U + n
                b, u = n // U, n % U
                dve.wait_ge(sem("scores_full"), N + 1)
                ps = scores_ps[:, N % 3, :].rearrange("p (k t) -> p k t", k=HU)
                if a in (2, 4) and n >= 3:
                    dve.wait_ge(sem("exp_done"), N - 2)
                if a == 2:
                    if n == 0:
                        dve.wait_ge(sem("mask1_in"), 16)
                    for k in range(HU):
                        ins = nc.vector.tensor_tensor_reduce(
                            out=masked[:, N % 3, k, :], in0=ps[:, k, :], in1=mask1[:, b, :],
                            scale=1.0, scalar=-3.4e38, op0=ALU.add, op1=ALU.max,
                            accum_out=posmax[:, N % 4, k:k + 1])
                    link(ins)
                    nc.vector.tensor_scalar(negmax[:, N % 4, :], posmax[:, N % 4, :], -1.0, None,
                                            ALU.mult).then_inc(sem("max_done"), 1)
                elif a == 4:
                    if u == 0:
                        read_out(dve, "mask4", b)
                    link(nc.vector.tensor_tensor(
                        masked[:, N % 3, :, :], ps,
                        fT[:, b, :].unsqueeze(1).to_broadcast([P, HU, S]), ALU.mult))
                    nc.vector.tensor_scalar(masked[:, N % 3, :, :], masked[:, N % 3, :, :], 50.0, -50.0,
                                            ALU.min, ALU.max).then_inc(sem("clipped"), 1)
                else:
                    nc.vector.tensor_reduce(negmax[:, N % 4, :], ps, AX.X, ALU.max,
                                            negate=True).then_inc(sem("max_done"), 1)

            def rotate(use, k, b):
                full = take(dve, use, b)
                heads = 8 if k < 2 else NKV
                cos, sin = (const("cosq"), const("sinq")) if k < 2 else (const("cosk"), const("sink"))
                if k == 2:
                    nc.vector.tensor_copy(v64[:, b, :, 0:HD],
                                          full[:, 256:512].rearrange("p (g d) -> p g d", g=NKV))
                    t1, t2 = res[:, b, :], zn[:, b, :]
                else:
                    t1, t2 = (wide[:, b, at:at + 512] for at in (k * 512, FF + k * 512))
                ps = full[:, 0:heads * HD].rearrange("p (h r d) -> p h r d", h=heads, r=2)
                t2 = t2.rearrange("p (h r d) -> p h r d", h=heads, r=2)
                nc.vector.tensor_tensor(t1.rearrange("p (h d) -> p h d", h=heads),
                                        ps.rearrange("p h r d -> p h (r d)"),
                                        cos.unsqueeze(1).to_broadcast([P, heads, HD]), ALU.mult)
                for r in range(2):
                    half = sin[:, r * 32:(r + 1) * 32].unsqueeze(1).to_broadcast([P, heads, 32])
                    ins = nc.vector.tensor_tensor(t2[:, :, r, :], ps[:, :, 1 - r, :], half, ALU.mult)
                release(ins, use, b)

            for name, a, i_ in events:
                b = i_
                if name == "scores":
                    scores_out(a, i_)
                elif name == "values" and a == 2:
                    b, u = i_ // U, i_ % U
                    dve.wait_ge(sem("values_done"), a * G * U + i_ + 1)
                    ps = pv_ps[:, 0:HU * VW1].rearrange("p (k w) -> p k w", k=HU)
                    link(nc.vector.reciprocal(rden[:, b, u * HU:(u + 1) * HU], ps[:, :, HD]))
                    nc.vector.tensor_tensor(
                        nat[:, b, u * D:(u + 1) * D].rearrange("p (k d) -> p k d", k=HU), ps[:, :, 0:HD],
                        rden[:, b, u * HU:(u + 1) * HU].unsqueeze(2).to_broadcast([P, HU, HD]), ALU.mult)\
                        .then_inc(sem("pv_read"), 1)
                elif name == "xT":
                    if b == 0:
                        dve.wait_ge(sem("x_in"), 16)
                    link(nonzero_rows(x_in[:, b, :], 0, b))
                elif name == "proj":
                    per_head(a, b)
                    if a < 2:
                        first_query(a, b)
                elif name == "first_row":
                    length_penalty(a, b)
                elif name == "ctx_norms":
                    if b == 0:
                        dve.wait_ge(sem("ctx_in"), 16)
                    link(nc.vector.bn_stats(cst[:, b, :], ctx[:, b, :]))
                    link(nc.vector.bn_aggr(cmv[:, b, :], cst[:, b, :]))
                    nc.vector.tensor_scalar(cve[:, b, 0:1], cmv[:, b, 1:2], 1e-5, None, ALU.add)
                    link(nc.vector.scalar_tensor_tensor(cve[:, b, 1:2], cmv[:, b, 0:1], cmv[:, b, 0:1],
                                                        cmv[:, b, 1:2], ALU.mult, ALU.add))
                    nc.vector.tensor_scalar(cve[:, b, 1:2], cve[:, b, 1:2], 1e-6, None, ALU.add)\
                        .then_inc(sem("cve"), 1)
                elif name == "attended":
                    normalized(a, b, which=a if a < 2 else None)
                elif name == "stats":
                    dve.wait_ge(sem(f"res_{a}"), b + 1)
                    statistics(res[:, b, :], b, 1e-5, f"ve_{a}")
                elif name == "norm" and a < 2:
                    layernorm(res[:, b, :], xs[:, b, :], f"ln{a + 1}g", f"ln{a + 1}b", b, f"rstd_{a}",
                              f"x{a + 1}")
                    if a == 0:
                        dve.wait_ge(sem("x1"), b + 1)
                        nonzero_rows(xs[:, b, :], 1, b).then_inc(sem("live1"), 1)
                elif name == "z":
                    ps = take(dve, "z", b)
                    release(nc.vector.tensor_tensor(zn[:, b, :], ps[:, 0:D], row("fc2b"), ALU.add), "z", b)
                    read_out(dve, "z", b)
                    link(nc.vector.scalar_tensor_tensor(res[:, b, :], zn[:, b, :], live[:, 0, b:b + 1],
                                                        xs[:, b, :], ALU.mult, ALU.add))
                    statistics(res[:, b, :], b, 1e-5, "ve_m")
                elif name == "norm_x3":
                    layernorm(res[:, b, :], xs[:, b, :], "ln3g", "ln3b", b, "rstd_m", "x3")
                elif name == "mean_square":
                    tag, sums = ("2", "ssq3") if a == 2 else ("h", "ssqh")
                    dve.wait_ge(sem(sums), b + 1)
                    nc.vector.tensor_scalar(ve[:, b, 0:1], ssq[:, b:b + 1], 1.0 / D, 1e-6, ALU.mult, ALU.add)\
                        .then_inc(sem(f"ve_{tag}"), 1)
                elif name == "rms_norm":
                    tag, signal = ("2", "n3") if a == 2 else ("h", "n_h")
                    dve.wait_ge(sem(f"rstd_{tag}"), b + 1)
                    nc.vector.tensor_scalar(zn[:, b, :], xs[:, b, :], rstd[:, b, 0:1], None, ALU.mult)\
                        .then_inc(sem(signal), 1)
                elif name == "q2":
                    rotate("q2a", 0, b)
                    rotate("q2b", 1, b)
                elif name == "kv2":
                    rotate("kv2", 2, b)
                elif name == "rotatedT":
                    ps = take(dve, "kT2", b)
                    release(nc.vector.tensor_copy(plainT[:, b, :, :].rearrange("p c s -> p (c s)"),
                                                  ps[:, 0:D]), "kT2", b)
                elif name == "aT" and a == 1:
                    ps = take(dve, "aT1", b)
                    release(nc.vector.tensor_copy(tr[:, b, 4:8, :].rearrange("p c s -> p (c s)"), ps),
                            "aT1", b)
                elif name == "o2":
                    ps = take(dve, "o2", b)
                    release(nc.vector.tensor_tensor(xs[:, b, :], ps[:, 0:D], xs[:, b, :], ALU.add), "o2", b)
                elif name == "gate_up":
                    half = nat[:, b, a * 512:(a + 1) * 512]
                    dve.wait_ge(sem("tanh"), 2 * b + a + 1)
                    ps = take(dve, f"g{a}", b)
                    release(nc.vector.scalar_tensor_tensor(half, half, 1.0, ps, ALU.add, ALU.mult),
                            f"g{a}", b)
                    read_out(dve, f"g{a}", b)
                    ps = take(dve, f"u{a}", b)
                    release(nc.vector.scalar_tensor_tensor(
                        tr[:, b, 4 * a:4 * a + 4, :].rearrange("p c s -> p (c s)"), half, 0.5, ps,
                        ALU.mult, ALU.mult), f"u{a}", b)
                elif name == "down":
                    ps = take(dve, "dn", b)
                    release(nc.vector.tensor_tensor(xs[:, b, :], ps[:, 0:D], xs[:, b, :], ALU.add), "dn", b)
                    read_out(dve, "dn", b)
                    statistics(xs[:, b, :], b, 1e-5, "ve_4")
                elif name == "norm_x4":
                    dve.wait_ge(sem("rstd_4"), b + 1)
                    nc.vector.tensor_scalar(zn[:, b, :], xs[:, b, :], mv[:, b, 0:1], rstd[:, b, 0:1],
                                            ALU.subtract, ALU.mult).then_inc(sem("n4"), 1)
                elif name == "mask4":
                    ps = take(dve, "mask4", b)
                    release(nc.vector.tensor_scalar(fT[:, b, :], ps[:, 0:S], 0.5, 0.5, ALU.mult, ALU.add),
                            "mask4", b)
                elif name == "o":
                    ps = take(dve, f"o{a}", b)
                    dve.wait_ge(sem(f"res_{a}"), b + 1)
                    release(nc.vector.tensor_tensor(xs[:, b, :], ps[:, 0:D], res[:, b, :], ALU.add),
                            f"o{a}", b)
                    if a == 4:
                        read_out(dve, "o4", b)
                        statistics(xs[:, b, :], b, 1e-5, "ve_5")
                elif name == "norm" and a == 4:
                    layernorm(xs[:, b, :], outn[:, b, :], "gamma", "beta", b, "rstd_5", "out_ready")

        first_x = x_d[0:G].rearrange("g s d -> s g d")
        next_x = x_d[G:B + G].rearrange("(n g) s d -> n s g d", g=G)
        ctx_g = ctx_d.rearrange("(n g) s d -> n s g d", g=G)
        mask1_g = mask1_d.rearrange("(n g) a s t -> n s g (a t)", g=G)
        mask3_g = mask3_d.rearrange("(n g) a s t -> n s g (a t)", g=G)
        out_g = out_d.rearrange("(n g) s d -> n s g d", g=G)

        setup_names = set(names)

        def clear_counts():
            for name in sorted(set(names) - setup_names | {n for n in names if n.startswith("bank_")}):
                nc.sync.sem_clear(names[name])
            with nc.Block() as block:
                @block.sync
                def _(sp):
                    sp.nop()

        plan.update(count_plan(PROLOGUE))
        with nc.Block() as block:
            @block.sync
            def _(sp):
                sp.dma_start(x_in[:, :, :], first_x).then_inc(sem("x_in"), 16)

            @block.tensor
            def _(pe):
                tensor_program(pe, PROLOGUE)

            @block.scalar
            def _(act):
                scalar_program(act, PROLOGUE)

            @block.vector
            def _(dve):
                vector_program(dve, PROLOGUE)

        clear_counts()
        plan.clear()
        plan.update(count_plan(SCHEDULE))
        with nc.Fori(0, NG) as i:
            with nc.Block() as block:
                @block.sync
                def _(sp):
                    sp.dma_start(ctx[:, :, :], ctx_g[i]).then_inc(sem("ctx_in"), 16)
                    sp.dma_start(mask1[:, :, :], mask1_g[i]).then_inc(sem("mask1_in"), 16)
                    sp.dma_start(mask3[:, :, :], mask3_g[i]).then_inc(sem("mask3_in"), 16)
                    bank, use = plan["tr2", G - 1]
                    sp.wait_ge(bank_full[bank], use)
                    sp.dma_start(x_in[:, :, :], next_x[i]).then_inc(sem("x_in"), 16)
                    for b in range(G):
                        sp.wait_ge(sem("out_ready"), b + 1)
                        sp.dma_start(out_g[i][:, b, :], outn[:, b, :]).then_inc(sem("stored"), 16)
                    sp.wait_ge(sem("stored"), 16 * G)

                @block.tensor
                def _(pe):
                    tensor_program(pe, SCHEDULE)

                @block.scalar
                def _(act):
                    scalar_program(act, SCHEDULE)

                @block.gpsimd
                def _(pool):
                    gpsimd_program(pool, SCHEDULE)

                @block.vector
                def _(dve):
                    vector_program(dve, SCHEDULE)

            clear_counts()


def pack(w):
    k, n = w.shape
    return w.reshape(k // P, P, n).transpose(1, 0, 2).reshape(P, -1)


def grouped_heads(w):
    return w.reshape(-1, 2, 2, 4, HD).transpose(0, 1, 3, 2, 4).reshape(-1, FF)


def by_head(w):
    return w.transpose(1, 0, 2).reshape(D, D)


def shape_constants():
    f = np.float32
    p = np.arange(P)
    inv_freq = (f(1.0) / f(10000.0) ** (np.arange(0, HD, 2, dtype=f) / f(HD))).astype(f)
    angle = p.astype(f)[:, None] * inv_freq[None, :]
    cos, sin = np.cos(angle), np.sin(angle)
    cos2, sin2 = np.concatenate([cos, cos], 1), np.concatenate([-sin, sin], 1)
    head8 = (p[:, None] // 16 == np.arange(8)[None, :]).astype(f)
    bd = np.zeros((P, C, C, 8), f)
    for c in range(C):
        bd[:, c, c, :] = head8
    parts = {"ident": np.eye(P, dtype=f), "causal": np.where(p[None, :] > p[:, None], f(MASKED), f(0.0)),
             "iota": np.broadcast_to(p.astype(f), (P, P)), "cosq": cos2 / f(8), "sinq": sin2 / f(8), "cosk": cos2,
             "sink": sin2, "head8": head8, "head8q": head8 * f(0.25),
             "bd": bd.reshape(P, -1), "expo": np.full((P, 2), -0.5, f)}
    return np.ascontiguousarray(np.concatenate([parts[n].astype(f) for n, _ in CONSTS], 1))


def kernel(**inputs):
    import concourse.bacc as bacc
    from concourse.bass_utils import run_bass_kernel_spmd

    a = {k: np.asarray(v) for k, v in inputs.items()}
    l0, l1, l2, l3 = "L0_xattn_", "L1_xattn_", "L2_xattn_", "L3_xattn_"
    cat = np.concatenate
    weights = {
        "qk0": cat([by_head(a[l0 + "Wq1"]), by_head(a[l0 + "Wk1"])], 1),
        "v0": by_head(a[l0 + "Wv1"]),
        "qk1": cat([by_head(a[l0 + "Wq2"]), by_head(a[l0 + "Wk2"])], 1),
        "v1": by_head(a[l0 + "Wv2"]), "fc1": a[l0 + "fc1_w"].T, "fc2": a[l0 + "fc2_w"].T,
        "q2": grouped_heads(a[l1 + "Wq"]), "kv2": cat([a[l1 + "Wk"], a[l1 + "Wv"]], 1), "o2": a[l1 + "Wo"],
        "gate": a[l1 + "Wgate"], "up": a[l1 + "Wup"], "down": a[l1 + "Wdown"],
        "qk3": cat([a[l2 + "Wq"], a[l2 + "Wk"]], 1), "v3": a[l2 + "Wv"],
        "o3": a[l2 + "Wo"],
        "qk4": cat([a[l3 + "Wq"], a[l3 + "Wk"]], 1), "v4": a[l3 + "Wv"],
        "o4": a[l3 + "Wo"]}
    rows = {"ln1g": a[l0 + "ln1_g"], "ln1b": a[l0 + "ln1_b"], "ln2g": a[l0 + "ln2_g"], "ln2b": a[l0 + "ln2_b"],
            "ln3g": a[l0 + "ln3_g"], "ln3b": a[l0 + "ln3_b"], "fc2b": a[l0 + "fc2_b"], "bo3": a[l2 + "bo"],
            "bo4": a[l3 + "bo"], "gamma": a[l3 + "gamma"], "beta": a[l3 + "beta"]}
    cols = {"fc1b": a[l0 + "fc1_b"], "rms1": a[l1 + "ln1_w"], "rms2": a[l1 + "ln2_w"],
            "bq3": a[l2 + "bq"], "bk3": a[l2 + "bk"],
            "bv3": a[l2 + "bv"], "gq": a[l2 + "gq"], "betaq": a[l2 + "betaq"], "gkv": a[l2 + "gkv"],
            "betakv": a[l2 + "betakv"], "bq4": a[l3 + "bq"],
            "bk4": a[l3 + "bk"], "bv4": a[l3 + "bv"]}
    arrays = {
        "x": cat([a["x"], a["x"][:G]], 0), "ctx": a["ctx_1024"], "mask1": a["mask_Bx1xSxS2_ff0"], "mask3": a["mask_Bx1xSxS2_fk0"],
        "weights": cat([pack(weights[n]) for n, _ in WEIGHTS], 1),
        "rows": np.broadcast_to(cat([rows[n] for n in ROWS])[None, :], (P, R_ALL)),
        "cols": cat([cols[n].reshape(C, P).T for n in COLS], 1),
        "consts": shape_constants()}
    arrays = {k: np.ascontiguousarray(v) for k, v in arrays.items()}

    nc = bacc.Bacc("TRN2", target_bir_lowering=False, num_devices=1)
    aps = [nc.dram_tensor(f"{k}_dram", v.shape, mybir.dt.from_np(v.dtype), kind="ExternalInput").ap() for k, v in arrays.items()]
    out = nc.dram_tensor("out_dram", (B, S, D), mybir.dt.float32, kind="ExternalOutput").ap()
    build(nc, *aps, out)
    r = run_bass_kernel_spmd(nc, [{f"{k}_dram": v for k, v in arrays.items()}], core_ids=[0])
    return r.results[0]["out_dram"]
```
